# Optimizing a Trainium2 kernel written in Bass

```python
import numpy as np
import jax
import jax.numpy as jnp

def _softmax(x, axis=-1):
    return jax.nn.softmax(x, axis=axis)

def _gelu(x):
    return jax.nn.gelu(x, approximate=True)

def _silu(x):
    return jax.nn.silu(x)

def _sigmoid(x):
    return jax.nn.sigmoid(x)

def _layernorm(x, axis=-1, eps=1e-05):
    m = jnp.mean(x, axis=axis, keepdims=True)
    v = jnp.var(x, axis=axis, keepdims=True)
    return (x - m) / jnp.sqrt(v + eps)

def _scatter_add(tgt, idx, src, axis=0):
    return tgt.at[idx].add(src)

def _segment_sum(src, seg, n):
    return jax.ops.segment_sum(src, seg, n)
kernel_name = 'mk_adaln_d1_jaxref_r8_0c4ae1'

def setup_inputs(seed: int=0):
    np.random.seed(seed)
    _w = jnp.asarray

    def _L0_attn_setup():
        import jax, jax.numpy as jnp
        import numpy as np
        D_MODEL = 128
        D_STATE = 128
        D_CONV = 4
        EXPAND = 2
        NHEADS = 32
        NGROUPS = 1
        D_INNER = EXPAND * D_MODEL
        HEADDIM = D_INNER // NHEADS
        CHUNK = 32
        BATCH, SEQLEN = (2, 256)
        D_IN_PROJ = 2 * D_INNER + 2 * NGROUPS * D_STATE + NHEADS
        CONV_DIM = D_INNER + 2 * NGROUPS * D_STATE
        LN_EPS = 1e-05

        def _segsum(x):
            T = x.shape[-1]
            cs = jnp.cumsum(x, axis=-1)
            diff = cs[..., :, None] - cs[..., None, :]
            mask = jnp.tril(jnp.ones((T, T), bool))
            return jnp.where(mask, diff, -jnp.inf)

        def _ssd_chunked(X, A, B, C, chunk):
            b, l, h, p = X.shape
            c = l // chunk
            X = X.reshape(b, c, chunk, h, p)
            B = B.reshape(b, c, chunk, h, -1)
            C = C.reshape(b, c, chunk, h, -1)
            A = A.reshape(b, c, chunk, h).transpose(0, 3, 1, 2)
            A_cs = jnp.cumsum(A, axis=-1)
            L = jnp.exp(_segsum(A))
            Y_diag = jnp.einsum('bclhn,bcshn,bhcls,bcshp->bclhp', C, B, L, X)
            decay_states = jnp.exp(A_cs[..., -1:] - A_cs)
            states = jnp.einsum('bclhn,bhcl,bclhp->bchpn', B, decay_states, X)
            states = jnp.concatenate([jnp.zeros_like(states[:, :1]), states], axis=1)
            decay_chunk = jnp.exp(_segsum(jnp.pad(A_cs[..., -1], ((0, 0), (0, 0), (1, 0)))))
            new_states = jnp.einsum('bhzc,bchpn->bzhpn', decay_chunk, states)
            states = new_states[:, :-1]
            Y_off = jnp.einsum('bclhn,bchpn,bhcl->bclhp', C, states, jnp.exp(A_cs))
            return (Y_diag + Y_off).reshape(b, l, h, p)
        key = jax.random.key(seed)
        ks = jax.random.split(key, 8)
        dt = jnp.exp(jax.random.uniform(ks[4], (NHEADS,)) * (np.log(0.1) - np.log(0.001)) + np.log(0.001))
        dt = jnp.clip(dt, 0.0001, None)
        inv_dt = dt + jnp.log(-jnp.expm1(-dt))
        A = jax.random.uniform(ks[5], (NHEADS,), minval=1.0, maxval=16.0)
        return {'u': jax.random.normal(ks[0], (BATCH, SEQLEN, D_MODEL), jnp.float32), 'in_proj_w': jax.random.normal(ks[1], (D_IN_PROJ, D_MODEL), jnp.float32) * D_MODEL ** (-0.5), 'conv_w': jax.random.normal(ks[2], (CONV_DIM, D_CONV), jnp.float32) * D_CONV ** (-0.5), 'conv_b': jnp.zeros((CONV_DIM,), jnp.float32), 'dt_bias': inv_dt.astype(jnp.float32), 'A_log': jnp.log(A).astype(jnp.float32), 'ln_w': jnp.ones((D_INNER,), jnp.float32), 'out_proj_w': jax.random.normal(ks[3], (D_MODEL, D_INNER), jnp.float32) * D_INNER ** (-0.5)}
    _L0_attn_in = _L0_attn_setup()

    def _L0_ffn_setup():
        import jax, jax.numpy as jnp
        import numpy as np
        EPS = 1e-05
        TOP_K = 2

        def _rmsnorm(x, w):
            xf = x.astype(jnp.float32)
            rms = jax.lax.rsqrt(jnp.mean(xf * xf, axis=-1, keepdims=True) + EPS)
            return (xf * rms).astype(x.dtype) * w

        def _attention(x, wq, wk, wv, wo, num_heads=16):
            B, S, H = x.shape
            D = H // num_heads
            q = (x @ wq.T).reshape(B, S, num_heads, D)
            k = (x @ wk.T).reshape(B, S, num_heads, D)
            v = (x @ wv.T).reshape(B, S, num_heads, D)
            scale = 1.0 / jnp.sqrt(jnp.float32(D)).astype(x.dtype)
            scores = jnp.einsum('bqhd,bkhd->bhqk', q, k) * scale
            probs = jax.nn.softmax(scores, axis=-1)
            out = jnp.einsum('bhqk,bkhd->bqhd', probs, v).reshape(B, S, H)
            return out @ wo.T

        def _moe(x, gate_w, w1, w2, w3):
            B, S, H = x.shape
            xf = x.reshape(-1, H)
            logits = xf @ gate_w.T
            rw, sel = jax.lax.top_k(logits, TOP_K)
            rw = jax.nn.softmax(rw.astype(jnp.float32), axis=-1).astype(x.dtype)
            E = gate_w.shape[0]
            out = jnp.zeros_like(xf)
            for e in range(E):
                we = jnp.sum(jnp.where(sel == e, rw, 0.0), axis=-1)
                h = jax.nn.silu(xf @ w1[e].T) * (xf @ w3[e].T)
                out = out + h @ w2[e].T * we[:, None]
            return out.reshape(B, S, H)
        key = jax.random.key(seed)
        ks = jax.random.split(key, 10)
        H, I, E, NH = (128, 256, 8, 16)
        B, S = (2, 256)
        s = 0.02
        return {'x': jax.random.normal(ks[0], (B, S, H), jnp.float32), 'ln1_w': jnp.ones((H,), jnp.float32), 'ln2_w': jnp.ones((H,), jnp.float32), 'wq': jax.random.normal(ks[1], (H, H), jnp.float32) * s, 'wk': jax.random.normal(ks[2], (H, H), jnp.float32) * s, 'wv': jax.random.normal(ks[3], (H, H), jnp.float32) * s, 'wo': jax.random.normal(ks[4], (H, H), jnp.float32) * s, 'gate_w': jax.random.normal(ks[5], (E, H), jnp.float32) * s, 'w1': jax.random.normal(ks[6], (E, I, H), jnp.float32) * s, 'w2': jax.random.normal(ks[7], (E, H, I), jnp.float32) * s, 'w3': jax.random.normal(ks[8], (E, I, H), jnp.float32) * s}
    _L0_ffn_in = _L0_ffn_setup()
    _L0_c = _w((lambda *s: np.random.randn(*s).astype(np.float32) * 0.05)(4, 128))
    _L0_wmod = _w((lambda *s: np.random.randn(*s).astype(np.float32) * 0.05)(128, 6 * 128) * 128 ** (-0.5))
    _d = {'L0_attn_u': _L0_attn_in['u'], 'L0_attn_in_proj_w': _L0_attn_in['in_proj_w'], 'L0_attn_conv_w': _L0_attn_in['conv_w'], 'L0_attn_conv_b': _L0_attn_in['conv_b'], 'L0_attn_dt_bias': _L0_attn_in['dt_bias'], 'L0_attn_A_log': _L0_attn_in['A_log'], 'L0_attn_ln_w': _L0_attn_in['ln_w'], 'L0_attn_out_proj_w': _L0_attn_in['out_proj_w'], 'L0_ffn_ln1_w': _L0_ffn_in['ln1_w'], 'L0_ffn_ln2_w': _L0_ffn_in['ln2_w'], 'L0_ffn_wq': _L0_ffn_in['wq'], 'L0_ffn_wk': _L0_ffn_in['wk'], 'L0_ffn_wv': _L0_ffn_in['wv'], 'L0_ffn_wo': _L0_ffn_in['wo'], 'L0_ffn_gate_w': _L0_ffn_in['gate_w'], 'L0_ffn_w1': _L0_ffn_in['w1'], 'L0_ffn_w2': _L0_ffn_in['w2'], 'L0_ffn_w3': _L0_ffn_in['w3'], 'L0_c': _L0_c, 'L0_wmod': _L0_wmod}
    _x0 = _d['L0_attn_u']
    _d['L0_attn_u'] = jax.random.normal(jax.random.fold_in(jax.random.key(seed), 1), (4, 1024, 128), dtype=_x0.dtype)
    del _x0
    return _d

def reference(L0_attn_u, L0_attn_in_proj_w, L0_attn_conv_w, L0_attn_conv_b, L0_attn_dt_bias, L0_attn_A_log, L0_attn_ln_w, L0_attn_out_proj_w, L0_ffn_ln1_w, L0_ffn_ln2_w, L0_ffn_wq, L0_ffn_wk, L0_ffn_wv, L0_ffn_wo, L0_ffn_gate_w, L0_ffn_w1, L0_ffn_w2, L0_ffn_w3, L0_c, L0_wmod):

    def _L0_attn_ref(u, in_proj_w, conv_w, conv_b, dt_bias, A_log, ln_w, out_proj_w):
        import jax, jax.numpy as jnp
        import numpy as np
        D_MODEL = 128
        D_STATE = 128
        D_CONV = 4
        EXPAND = 2
        NHEADS = 32
        NGROUPS = 1
        D_INNER = EXPAND * D_MODEL
        HEADDIM = D_INNER // NHEADS
        CHUNK = 32
        BATCH, SEQLEN = (2, 256)
        D_IN_PROJ = 2 * D_INNER + 2 * NGROUPS * D_STATE + NHEADS
        CONV_DIM = D_INNER + 2 * NGROUPS * D_STATE
        LN_EPS = 1e-05

        def _segsum(x):
            T = x.shape[-1]
            cs = jnp.cumsum(x, axis=-1)
            diff = cs[..., :, None] - cs[..., None, :]
            mask = jnp.tril(jnp.ones((T, T), bool))
            return jnp.where(mask, diff, -jnp.inf)

        def _ssd_chunked(X, A, B, C, chunk):
            b, l, h, p = X.shape
            c = l // chunk
            X = X.reshape(b, c, chunk, h, p)
            B = B.reshape(b, c, chunk, h, -1)
            C = C.reshape(b, c, chunk, h, -1)
            A = A.reshape(b, c, chunk, h).transpose(0, 3, 1, 2)
            A_cs = jnp.cumsum(A, axis=-1)
            L = jnp.exp(_segsum(A))
            Y_diag = jnp.einsum('bclhn,bcshn,bhcls,bcshp->bclhp', C, B, L, X)
            decay_states = jnp.exp(A_cs[..., -1:] - A_cs)
            states = jnp.einsum('bclhn,bhcl,bclhp->bchpn', B, decay_states, X)
            states = jnp.concatenate([jnp.zeros_like(states[:, :1]), states], axis=1)
            decay_chunk = jnp.exp(_segsum(jnp.pad(A_cs[..., -1], ((0, 0), (0, 0), (1, 0)))))
            new_states = jnp.einsum('bhzc,bchpn->bzhpn', decay_chunk, states)
            states = new_states[:, :-1]
            Y_off = jnp.einsum('bclhn,bchpn,bhcl->bclhp', C, states, jnp.exp(A_cs))
            return (Y_diag + Y_off).reshape(b, l, h, p)
        b, l, _ = u.shape
        zxbcdt = u @ in_proj_w.T
        z = zxbcdt[..., :D_INNER]
        xBC = zxbcdt[..., D_INNER:D_INNER + CONV_DIM]
        dt = jax.nn.softplus(zxbcdt[..., -NHEADS:] + dt_bias)
        A = -jnp.exp(A_log)
        xp = jnp.pad(xBC, ((0, 0), (D_CONV - 1, 0), (0, 0)))
        acc = conv_b
        for k in range(D_CONV):
            acc = acc + xp[:, k:k + l, :] * conv_w[:, k]
        xBC = jax.nn.silu(acc)
        x = xBC[..., :D_INNER].reshape(b, l, NHEADS, HEADDIM)
        Bm = xBC[..., D_INNER:D_INNER + NGROUPS * D_STATE].reshape(b, l, NGROUPS, D_STATE)
        Cm = xBC[..., D_INNER + NGROUPS * D_STATE:].reshape(b, l, NGROUPS, D_STATE)
        rep = NHEADS // NGROUPS
        Bh = jnp.repeat(Bm, rep, axis=2)
        Ch = jnp.repeat(Cm, rep, axis=2)
        y = _ssd_chunked(x * dt[..., None], A * dt, Bh, Ch, CHUNK)
        y = y.reshape(b, l, D_INNER)
        mu = y.mean(-1, keepdims=True)
        var = y.var(-1, keepdims=True)
        y = (y - mu) / jnp.sqrt(var + LN_EPS) * ln_w
        y = y * jax.nn.silu(z)
        return y @ out_proj_w.T

    def _L0_ffn_ref(x, ln1_w, ln2_w, wq, wk, wv, wo, gate_w, w1, w2, w3):
        import jax, jax.numpy as jnp
        import numpy as np
        EPS = 1e-05
        TOP_K = 2

        def _rmsnorm(x, w):
            xf = x.astype(jnp.float32)
            rms = jax.lax.rsqrt(jnp.mean(xf * xf, axis=-1, keepdims=True) + EPS)
            return (xf * rms).astype(x.dtype) * w

        def _attention(x, wq, wk, wv, wo, num_heads=16):
            B, S, H = x.shape
            D = H // num_heads
            q = (x @ wq.T).reshape(B, S, num_heads, D)
            k = (x @ wk.T).reshape(B, S, num_heads, D)
            v = (x @ wv.T).reshape(B, S, num_heads, D)
            scale = 1.0 / jnp.sqrt(jnp.float32(D)).astype(x.dtype)
            scores = jnp.einsum('bqhd,bkhd->bhqk', q, k) * scale
            probs = jax.nn.softmax(scores, axis=-1)
            out = jnp.einsum('bhqk,bkhd->bqhd', probs, v).reshape(B, S, H)
            return out @ wo.T

        def _moe(x, gate_w, w1, w2, w3):
            B, S, H = x.shape
            xf = x.reshape(-1, H)
            logits = xf @ gate_w.T
            rw, sel = jax.lax.top_k(logits, TOP_K)
            rw = jax.nn.softmax(rw.astype(jnp.float32), axis=-1).astype(x.dtype)
            E = gate_w.shape[0]
            out = jnp.zeros_like(xf)
            for e in range(E):
                we = jnp.sum(jnp.where(sel == e, rw, 0.0), axis=-1)
                h = jax.nn.silu(xf @ w1[e].T) * (xf @ w3[e].T)
                out = out + h @ w2[e].T * we[:, None]
            return out.reshape(B, S, H)
        h = x + _attention(_rmsnorm(x, ln1_w), wq, wk, wv, wo)
        h = h + _moe(_rmsnorm(h, ln2_w), gate_w, w1, w2, w3)
        return h
    x = L0_attn_u
    mod = (_silu(L0_c) @ L0_wmod).reshape(L0_c.shape[0], 6, 1, -1)
    sa, ca, ga, sb, cb, gb = (mod[:, 0], mod[:, 1], mod[:, 2], mod[:, 3], mod[:, 4], mod[:, 5])
    ga = (2 * (ga >= 0) - 1) * jnp.maximum(jnp.abs(ga), 0.25)
    gb = (2 * (gb >= 0) - 1) * jnp.maximum(jnp.abs(gb), 0.25)
    h = _layernorm(x, axis=-1) * (1 + ca) + sa
    x = x + ga * _L0_attn_ref(h, L0_attn_in_proj_w, L0_attn_conv_w, L0_attn_conv_b, L0_attn_dt_bias, L0_attn_A_log, L0_attn_ln_w, L0_attn_out_proj_w)
    h = _layernorm(x, axis=-1) * (1 + cb) + sb
    x = x + gb * _L0_ffn_ref(h, L0_ffn_ln1_w, L0_ffn_ln2_w, L0_ffn_wq, L0_ffn_wk, L0_ffn_wv, L0_ffn_wo, L0_ffn_gate_w, L0_ffn_w1, L0_ffn_w2, L0_ffn_w3)
    return x

_drawn_inputs = setup_inputs


def setup_inputs(seed=0):
    import zlib

    import numpy as np

    out = dict(_drawn_inputs(seed))
    spreads = {'L0_attn_conv_b': (0.0, 0.1),
     'L0_attn_ln_w': (1.0, 0.2),
     'L0_ffn_ln1_w': (1.0, 0.6),
     'L0_ffn_ln2_w': (1.0, 0.6)}
    factors = {'L0_ffn_wq': 8.0,
     'L0_ffn_wk': 8.0,
     'L0_ffn_wv': 8.0,
     'L0_ffn_wo': 8.0,
     'L0_ffn_gate_w': 8.0,
     'L0_ffn_w1': 8.0,
     'L0_ffn_w2': 8.0,
     'L0_ffn_w3': 8.0}
    for name, (base, spread) in spreads.items():
        noise = np.random.default_rng([zlib.crc32(name.encode()), seed]).standard_normal(out[name].shape)
        drawn = base * np.exp(spread * noise) if base else spread * noise
        out[name] = jnp.asarray(drawn.astype(out[name].dtype))
    for name, factor in factors.items():
        out[name] = (out[name] * factor).astype(out[name].dtype)
    return out
```

```python
from contextlib import ExitStack

import concourse.bass as bass
from concourse import mybir

F32 = mybir.dt.float32
BF16 = mybir.dt.bfloat16
U32 = mybir.dt.uint32
ALU = mybir.AluOpType
ACT = mybir.ActivationFunctionType
AXX = mybir.AxisListType.X

P = 128
B, L, D = 4, 1024, 128
NT = L // P
TILES = B * NT
NH, HP, DI, DS = 32, 8, 256, 128
PROJ = 2 * DI + 2 * DS + NH
TAPS = 4
AH, AD = 16, 8
HG = AH // 4
NE, FF = 8, 256
LN_EPS, RMS_EPS = 1e-5, 1e-5
GATE_MIN = 0.25
SCALE = float(AD) ** -0.5

Z0, XBC0, DT0 = 0, DI, 2 * DI + 2 * DS
BLOCKS = (2, 3, 0, 1)
Q_PART = (0, 1, 0, 2, 0, 1)
K_PART = (0, 0, 1, 0, 2, 1)
STACK = 8
MAX_ROW = 6


class Steps:

    def __init__(self, engine, order, base):
        self.engine, self.order, self.base, self.n = engine, order, base, 0

    def add(self, instruction):
        self.n += 1
        instruction.then_inc(self.order, 1)

    def settle(self):
        self.engine.wait_ge(self.order, self.base + self.n)


def spread(ap, n):
    return ap.unsqueeze(2).to_broadcast([ap.shape[0], ap.shape[1], n])


def repeat(ap, n):
    return ap.unsqueeze(1).to_broadcast([ap.shape[0], n, ap.shape[1]])


def state_space_and_qkv(nc, w, keep, scratch):
    ctx = ExitStack()
    with ctx:
        def sb(name, shape, dt=F32):
            return ctx.enter_context(nc.sbuf_tensor(name, shape, dt))

        def sem(name):
            return ctx.enter_context(nc.semaphore(name))

        bank = ctx.enter_context(nc.psum_tensor("bank_a", [P, 8, 512], F32))
        x_all, h2_all = keep["x_all"], keep["h2_all"]
        gate_rows = keep["gate_rows"]
        ident = keep["ident"]

        w_in = sb("w_in", [P, PROJ])
        w_out = sb("w_out", [P, 2, D])
        w_out_b = sb("w_out_b", [P, B, 2, D])
        w_qkv = sb("w_qkv", [P, 3, D])
        w_modT = sb("w_modT", [P, 6 * D])
        c_col = sb("c_col", [P, B])
        c_silu = sb("c_silu", [P, B])
        scale1 = sb("scale1", [P, B])
        shift1 = sb("shift1", [P, B])
        ln_w_col = sb("ln_w_col", [P, 2])
        rms1_col = sb("rms1_col", [P, 1])
        conv_w = sb("conv_w", [P, 4, TAPS])
        conv_b = sb("conv_b", [P, 4])
        dt_bias = sb("dt_bias", [P, NH])
        neg_A = sb("neg_A", [P, NH])
        eps_col = sb("eps_col", [P, 1])
        tri = sb("tri", [P, 3, P])
        ident_h = sb("ident_h", [P, P], BF16)
        neg_mask = sb("neg_mask", [P, P], BF16)
        gate_sign = sb("gate_sign", [P, B, D])

        stats1 = sb("stats1", [P, TILES, 6])
        mean1 = sb("mean1", [P, TILES, 2])
        rstd1 = sb("rstd1", [P, TILES])
        xn = sb("xn", [P, B, D])
        hT = sb("hT", [P, B, P])
        dt_v = sb("dt_v", [P, B * NH])
        dt_abs = sb("dt_abs", [P, B * NH])
        dt_u = sb("dt_u", [P, B * NH])
        dt_w = sb("dt_w", [P, B * NH])
        dt_ln = sb("dt_ln", [P, B * NH])
        dt_c = sb("dt_c", [P, B * NH])
        dt_r = sb("dt_r", [P, B * NH])
        dt = sb("dt", [P, B * NH])
        dta = sb("dta", [P, B * NH])
        decays = sb("decays", [P, 3, B * NH])
        cs_part = sb("cs_part", [P, 3, P], BF16)
        cs_rest = sb("cs_rest", [P, 2, P])
        seg_lhs = sb("seg_lhs", [P, B, P], BF16)
        seg_rhs = sb("seg_rhs", [P, B, NH * P], BF16)
        pre = sb("pre", [P, 4, B, TAPS - 1 + P])
        conv = sb("conv", [P, 4, B, P])
        xc = sb("xc", [P, 4, B, P])
        z_gate = sb("z_gate", [P, B, DI])
        rows = sb("rows", [P, 2, 4, P])
        x_dt = sb("x_dt", [P, 2, DI])
        x_ds = sb("x_ds", [P, 2, DI])
        seg = sb("seg", [P, 2, 4 * P])
        mix = sb("mix", [P, 2, 4, P])
        state = sb("state", [P, B, DI])
        y_off = sb("y_off", [P, DI])
        y = sb("y", [P, B, DI])
        stats_y = sb("stats_y", [P, B, 6])
        mean_y = sb("mean_y", [P, B, 2])
        rstd_y = sb("rstd_y", [P, B])
        yT = sb("yT", [P, B, 2, P])
        stats2 = sb("stats2", [P, B, 6])
        mean2 = sb("mean2", [P, B, 2])
        rstd2 = sb("rstd2", [P, B])
        h2 = sb("h2", [P, B, D])
        squares = sb("squares", [P, B, D])
        sumsq = sb("sumsq", [P, B])
        rms = sb("rms", [P, B])
        n2T = sb("n2T", [P, B, P])
        qk = sb("qk", [P, 2, B * P])
        qk_part = sb("qk_part", [P, 3, 2, B * P], BF16)
        qk_rest = sb("qk_rest", [P, 2, B * P])
        v_rows = sb("v_rows", [P, B, D])

        loaded = sem("loaded")
        x_loaded = sem("x_loaded")
        dve_order = sem("dve_order_a")
        act_order = sem("act_order_a")
        pool_order = sem("pool_order_a")
        sp_turn = sem("sp_turn_a")
        dve_turn = sem("dve_turn_a")
        zeroed = sem("zeroed")
        c_ready = sem("c_ready")
        mod_ready = sem("mod_ready")
        mod_read = sem("mod_read")
        stats1_ready = sem("stats1_ready")
        rstd1_ready = sem("rstd1_ready")
        negA_ready = sem("negA_ready")
        xn_ready = sem("xn_ready")
        xnT_ready = sem("xnT_ready")
        hT_ready = sem("hT_ready")
        dtraw_ready = sem("dtraw_ready")
        v_ready = sem("v_ready")
        u_ready = sem("u_ready")
        w_ready = sem("w_ready")
        ln_ready = sem("ln_ready")
        dta_ready = sem("dta_ready")
        xbc_ready = sem("xbc_ready")
        pre_ready = sem("pre_ready")
        halo_ready = sem("halo_ready")
        z_ready = sem("z_ready")
        zgate_ready = sem("zgate_ready")
        conv_ready = sem("conv_ready")
        xc_ready = sem("xc_ready")
        sums_ready = sem("sums_ready")
        csT_ready = sem("csT_ready")
        decays_ready = sem("decays_ready")
        parts_ready = sem("parts_ready")
        seg_built = sem("seg_built")
        turned_ready = sem("turned_ready")
        rows_ready = sem("rows_ready")
        xds_ready = sem("xds_ready")
        diff_ready = sem("diff_ready")
        seg_ready = sem("seg_ready")
        mix_ready = sem("mix_ready")
        ydiag_ready = sem("ydiag_ready")
        yoff_ready = sem("yoff_ready")
        y_ready = sem("y_ready")
        ystat_ready = sem("ystat_ready")
        yr_ready = sem("yr_ready")
        g_ready = sem("g_ready")
        gT_ready = sem("gT_ready")
        yT_ready = sem("yT_ready")
        out_ready = sem("out_ready")
        stat2_ready = sem("stat2_ready")
        r2_ready = sem("r2_ready")
        h2_ready = sem("h2_ready")
        rms_ready = sem("rms_ready")
        n2_ready = sem("n2_ready")
        n2T_ready = sem("n2T_ready")
        n2Ts_ready = sem("n2Ts_ready")
        qkv_ready = sem("qkv_ready")
        v_copied = sem("v_copied")
        x1_ready = sem("x1_ready")
        pool_turn = sem("pool_turn_a")
        qk_copied = sem("qk_copied")
        split_ready = sem("split_ready")
        qk_stored = sem("qk_stored")
        v_stored = sem("v_stored")
        pads_stored = sem("pads_stored")

        xd = w["u"].rearrange("b (t p) d -> p (b t) d", p=P)
        q_stack = scratch["q"].rearrange("b h d c s -> (h d) b c s")
        k_stack = scratch["k"].rearrange("b h d c s -> (h d) b c s")
        v_scr = scratch["v"].rearrange("b g p t c -> p b g t c")
        small_loads = [
            (c_col[:], w["c_T"]), (w_modT[:], w["wmod"]),
            (w_in[:], w["in_proj_T"]), (w_out[:], w["out_proj_T"].rearrange("(k p) n -> p k n", p=P)),
            (w_qkv[:, 0, :], w["wq_T"]), (w_qkv[:, 1, :], w["wk_T"]), (w_qkv[:, 2, :], w["wv_T"]),
            (ln_w_col[:], w["ln_w_cols"]),
            (rms1_col[:], w["ln1_col"]),
            (conv_w[:], w["conv_w"].rearrange("(k p) j -> p k j", p=P)),
            (conv_b[:], w["conv_b_cols"]),
            (dt_bias[:], w["dt_bias"].partition_broadcast(P)), (neg_A[:], w["A_log"].partition_broadcast(P)),
            (ident[:], w["ident"]), (ident_h[:], w["ident_h"]), (neg_mask[:], w["neg_mask"]),
            (tri[:], w["tri"].rearrange("k p n -> p k n")),
            (seg_lhs[3 * NH:3 * NH + 3, :, :], w["ones_h"].rearrange("k (b s) -> k b s", b=B)),
        ] + [(seg_rhs[0:3 * NH, b, :], w["neg_delta"]) for b in range(B)]
        LOADED = 16 * len(small_loads)

        block = ctx.enter_context(nc.Block())

        @block.sync
        def _(sp):
            for b in range(B):
                sp.dma_start(x_all[:, b * NT:(b + 1) * NT, :], xd[:, b * NT:(b + 1) * NT, :]).then_inc(x_loaded, 16)
            for dst, src in small_loads:
                sp.dma_start(dst, src).then_inc(loaded, 16)
            for b in range(B):
                sp.dma_start(q_stack[:, b, MAX_ROW:, :], w["q_pad"]).then_inc(pads_stored, 16)
                sp.dma_start(k_stack[:, b, MAX_ROW:, :], w["k_pad"]).then_inc(pads_stored, 16)
            with sp.Fori(0, NT) as t:
                sp.wait_ge(parts_ready, t + 1)
                sp.sem_inc(sp_turn, 1)
                for k in range(3):
                    sp.dma_start(seg_rhs[3 * NH + k:3 * NH + k + 1, :, :], cs_part[:, k, :]).then_inc(seg_built, 16)
                    for b in range(B):
                        sp.dma_start(seg_lhs[NH * k:NH * (k + 1), b, :],
                                     cs_part[NH * b:NH * (b + 1), k, :]).then_inc(seg_built, 16)
                sp.wait_ge(split_ready, t + 2)
                sp.sem_inc(sp_turn, 1)
                for c in range(MAX_ROW):
                    sp.dma_start(q_stack[:, :, c, bass.ds(t * P, P)],
                                 qk_part[:, Q_PART[c], 0, :].rearrange("p (b s) -> p b s", b=B)).then_inc(qk_stored, 16)
                    sp.dma_start(k_stack[:, :, c, bass.ds(t * P, P)],
                                 qk_part[:, K_PART[c], 1, :].rearrange("p (b s) -> p b s", b=B)).then_inc(qk_stored, 16)
                sp.wait_ge(v_copied, t + 1)
                sp.sem_inc(sp_turn, 1)
                sp.dma_start(v_scr[:, :, :, t, :],
                             v_rows[:].rearrange("p b (g c) -> p b g c", g=HG)).then_inc(v_stored, 16)
            sp.wait_ge(qk_stored, 16 * 2 * MAX_ROW * (NT + 1))
            sp.wait_ge(v_stored, 16 * (NT + 1))
            sp.wait_ge(pads_stored, 16 * 2 * B)
            sp.wait_ge(seg_built, 16 * 15 * NT)

        @block.scalar
        def _(act):
            A = nc.scalar.activation
            act.wait_ge(loaded, LOADED)
            A(c_silu[:], c_col[:], ACT.Silu).then_inc(c_ready, 1)
            A(neg_A[:], neg_A[:], ACT.Exp).then_inc(act_order, 1)
            act.wait_ge(act_order, 1)
            nc.scalar.mul(neg_A[:], neg_A[:], -1.0).then_inc(negA_ready, 1)
            act.wait_ge(zeroed, 1)
            act.wait_ge(stats1_ready, 1)
            A(rstd1[:], mean1[:, :, 1], ACT.Ln, bias=eps_col[:]).then_inc(act_order, 1)
            act.wait_ge(act_order, 2)
            A(rstd1[:], rstd1[:], ACT.Exp, scale=-0.5).then_inc(rstd1_ready, 1)
            act.wait_ge(mod_read, 2)
            act.wait_ge(loaded, LOADED)
            ACT_STEPS = 4
            with act.Fori(0, NT) as t:
                s = Steps(act, act_order, t * ACT_STEPS + 2)
                act.wait_ge(xnT_ready, t + 2)
                for b in range(B):
                    last = A(hT[:, b, :], bank[:, 0, b * P:(b + 1) * P], ACT.Identity,
                             scale=scale1[:, b:b + 1], bias=shift1[:, b:b + 1])
                last.then_inc(hT_ready, 1)
                act.wait_ge(v_ready, t + 1)
                A(dt_u[:], dt_abs[:], ACT.Exp, scale=-1.0).then_inc(u_ready, 1)
                act.wait_ge(w_ready, t + 1)
                A(dt_ln[:], dt_w[:], ACT.Ln).then_inc(ln_ready, 1)
                act.wait_ge(halo_ready, t + 1)
                for j in range(4):
                    act.wait_ge(xbc_ready, t * 4 + j + 1)
                    nc.scalar.copy(pre[:, BLOCKS[j], :, TAPS - 1:],
                                   bank[:, 1 + j % 2, :].rearrange("p (b s) -> p b s", b=B)).then_inc(pre_ready, 1)
                act.wait_ge(sums_ready, t + 1)
                A(decays[:].rearrange("p k c -> p (k c)"), bank[:, 1, 0:3 * P], ACT.Exp).then_inc(decays_ready, 1)
                for k in range(2):
                    act.wait_ge(z_ready, t * 2 + k + 1)
                    A(z_gate[:, 2 * k:2 * k + 2, :], bank[:, 3 * k, :], ACT.Silu).then_inc(zgate_ready, 1)
                for j in range(4):
                    act.wait_ge(conv_ready, t * 4 + j + 1)
                    A(xc[:, BLOCKS[j], :, :], conv[:, BLOCKS[j], :, :], ACT.Silu).then_inc(xc_ready, 1)
                for b in range(B):
                    act.wait_ge(turned_ready, t * B + b + 1)
                    nc.scalar.copy(rows[:, b % 2, :, :],
                                   bank[:, 7 - 7 * (b % 2), :].rearrange("p (k s) -> p k s", k=4)).then_inc(rows_ready, 1)
                    for q in range(8):
                        act.wait_ge(diff_ready, t * 32 + b * 8 + q + 1)
                        act.wait_ge(mix_ready, t * 32 + b * 8 + q + 1)
                        A(seg[:, q % 2, :], bank[:, 4 + q % 2, :], ACT.Exp).then_inc(seg_ready, 1)
                act.wait_ge(ystat_ready, t + 1)
                s.add(A(rstd_y[:], mean_y[:, :, 1], ACT.Ln, bias=eps_col[:]))
                s.settle()
                A(rstd_y[:], rstd_y[:], ACT.Exp, scale=-0.5).then_inc(yr_ready, 1)
                for k in range(2):
                    act.wait_ge(gT_ready, t * 2 + k + 1)
                    nc.scalar.copy(yT[:, 2 * k:2 * k + 2, :, :].rearrange("p b k s -> p (b k s)"),
                                   bank[:, 7 - 7 * k, :]).then_inc(yT_ready, 1)
                act.wait_ge(stat2_ready, t + 1)
                s.add(A(rstd2[:], mean2[:, :, 1], ACT.Ln, bias=eps_col[:]))
                s.settle()
                A(rstd2[:], rstd2[:], ACT.Exp, scale=-0.5).then_inc(r2_ready, 1)
                act.wait_ge(h2_ready, t + 1)
                for b in range(B):
                    last = A(squares[:, b, :], h2[:, b, :], ACT.Square, accum_out=sumsq[:, b:b + 1])
                s.add(last)
                s.settle()
                s.add(A(rms[:], sumsq[:], ACT.Ln, scale=1.0 / D, bias=eps_col[:]))
                s.settle()
                A(rms[:], rms[:], ACT.Exp, scale=-0.5).then_inc(rms_ready, 1)
                act.wait_ge(n2T_ready, t + 1)
                A(n2T[:].rearrange("p b s -> p (b s)"), bank[:, 7, :], ACT.Copy,
                  scale=rms1_col[:, 0:1]).then_inc(n2Ts_ready, 1)
                act.wait_ge(qkv_ready, t + 1)
                act.wait_ge(split_ready, t + 1)
                nc.scalar.mul(qk[:, 0, :], bank[:, 1, :], SCALE).then_inc(qk_copied, 1)
                nc.scalar.copy(qk[:, 1, :], bank[:, 2, :]).then_inc(qk_copied, 1)
                act.wait_ge(v_stored, 16 * (t + 1))
                nc.scalar.copy(v_rows[:].rearrange("p b c -> p (b c)"), bank[:, 6, :]).then_inc(v_copied, 1)
                assert s.n == ACT_STEPS

        @block.gpsimd
        def _(pool):
            pool.sem_inc(split_ready, 1)
            pool.sem_inc(v_stored, 16)
            pool.sem_inc(qk_stored, 16 * 2 * MAX_ROW)
            POOL_STEPS = 3
            with pool.Fori(0, NT) as t:
                s = Steps(pool, pool_order, t * POOL_STEPS)
                pool.wait_ge(qk_copied, t * 2 + 2)
                pool.sem_inc(pool_turn, 1)
                pool.wait_ge(qk_stored, 16 * 2 * MAX_ROW * (t + 1))
                pool.sem_inc(pool_turn, 1)
                s.add(nc.gpsimd.tensor_copy(qk_part[:, 0, :, :], qk[:]))
                s.settle()
                s.add(nc.gpsimd.tensor_tensor(qk_rest[:], qk[:], qk_part[:, 0, :, :], ALU.subtract))
                s.settle()
                pool.sem_inc(pool_turn, 1)
                s.add(nc.gpsimd.tensor_copy(qk_part[:, 1, :, :], qk_rest[:]))
                s.settle()
                nc.gpsimd.tensor_tensor(qk_part[:, 2, :, :], qk_rest[:], qk_part[:, 1, :, :],
                                        ALU.subtract).then_inc(split_ready, 1)
                assert s.n == POOL_STEPS

        @block.vector
        def _(dve):
            V = nc.vector
            V.memset(eps_col[:], LN_EPS)
            V.memset(pre[:, :, :, 0:TAPS - 1], 0.0)
            V.memset(state[:], 0.0).then_inc(zeroed, 1)
            dve.wait_ge(x_loaded, 16 * B)
            for i in range(TILES):
                last = V.bn_stats(stats1[:, i, :], x_all[:, i, :])
            last.then_inc(dve_order, 1)
            dve.wait_ge(dve_order, 1)
            for i in range(TILES):
                last = V.bn_aggr(mean1[:, i, :], stats1[:, i, :])
            last.then_inc(stats1_ready, 1)
            dve.wait_ge(c_ready, 1)
            for b in range(B):
                last = V.tensor_copy(xn[:, b, :], c_silu[:, b:b + 1].to_broadcast([P, P]))
            last.then_inc(c_ready, 1)
            dve.wait_ge(mod_ready, 1)
            V.tensor_copy(shift1[:], bank[:, 6, 0:B])
            V.tensor_scalar(scale1[:], bank[:, 6, B:2 * B], 1.0, None, ALU.add)
            for b in range(B):
                last = V.tensor_copy(gate_rows[:, b, :], bank[:, b, :])
            last.then_inc(mod_read, 1)
            dve.wait_ge(mod_read, 1)
            V.tensor_scalar(gate_rows[:, :, 2 * D:3 * D], gate_rows[:, :, 2 * D:3 * D], 1.0, None, ALU.add)
            order = 1
            for g in (0, 3):
                gate = gate_rows[:, :, g * D:(g + 1) * D]
                V.tensor_scalar(gate_sign[:], gate, 0.0, 2.0, ALU.is_ge, ALU.mult).then_inc(dve_order, 1)
                order += 1
                dve.wait_ge(dve_order, order)
                V.scalar_tensor_tensor(out=gate, in0=gate, scalar=-1.0, in1=gate, op0=ALU.mult,
                                       op1=ALU.max).then_inc(dve_order, 1)
                order += 1
                dve.wait_ge(dve_order, order)
                V.tensor_scalar(gate, gate, GATE_MIN, None, ALU.max).then_inc(dve_order, 1)
                order += 1
                dve.wait_ge(dve_order, order)
                V.scalar_tensor_tensor(out=gate, in0=gate_sign[:], scalar=-1.0, in1=gate, op0=ALU.add,
                                       op1=ALU.mult).then_inc(dve_order, 1)
                order += 1
                dve.wait_ge(dve_order, order)
            dve.wait_ge(loaded, LOADED)
            for b in range(B):
                for k in range(2):
                    last = V.scalar_tensor_tensor(out=w_out_b[:, b, k, :], in0=w_out[:, k, :],
                                                  scalar=ln_w_col[:, k:k + 1], in1=gate_rows[:, b, 0:D],
                                                  op0=ALU.mult, op1=ALU.mult)
            last.then_inc(mod_read, 1)
            dve.sem_inc(halo_ready, 1)
            dve.sem_inc(mix_ready, 2)
            dve.sem_inc(x1_ready, 1)
            dve.wait_ge(rstd1_ready, 1)
            dve.wait_ge(negA_ready, 1)
            DVE_STEPS = 45
            with dve.Fori(0, NT) as t:
                s = Steps(dve, dve_order, t * DVE_STEPS + order)

                def then_settle(instruction):
                    s.add(instruction)
                    s.settle()

                dve.wait_ge(xnT_ready, t + 1)
                for b in range(B):
                    i = b * NT + t
                    V.tensor_scalar(xn[:, b, :], x_all[:, i, :], mean1[:, i, 0:1], rstd1[:, bass.ds(i, 1)],
                                    ALU.subtract, ALU.mult).then_inc(xn_ready, 1)
                dve.wait_ge(dtraw_ready, t + 1)
                then_settle(V.tensor_tensor(dt_v[:].rearrange("p (b h) -> p b h", b=B),
                                            bank[:, 3, 0:P].rearrange("p (b h) -> p b h", b=B),
                                            repeat(dt_bias[:], B), ALU.add))
                V.scalar_tensor_tensor(out=dt_abs[:], in0=dt_v[:], scalar=-1.0, in1=dt_v[:], op0=ALU.mult,
                                       op1=ALU.max).then_inc(v_ready, 1)
                dve.wait_ge(u_ready, t + 1)
                V.tensor_scalar(dt_w[:], dt_u[:], 1.0, None, ALU.add).then_inc(w_ready, 1)
                dve.wait_ge(w_ready, t + 1)
                s.add(V.reciprocal(dt_r[:], dt_w[:]))
                then_settle(V.scalar_tensor_tensor(out=dt_c[:], in0=dt_w[:], scalar=-1.0, in1=dt_u[:],
                                                   op0=ALU.add, op1=ALU.subtract))
                then_settle(V.tensor_tensor(dt_c[:], dt_c[:], dt_r[:], ALU.mult))
                dve.wait_ge(ln_ready, t + 1)
                then_settle(V.scalar_tensor_tensor(out=dt[:], in0=dt_v[:], scalar=0.0, in1=dt_ln[:],
                                                   op0=ALU.max, op1=ALU.add))
                then_settle(V.tensor_tensor(dt[:], dt[:], dt_c[:], ALU.subtract))
                V.tensor_tensor(dta[:].rearrange("p (b h) -> p b h", b=B), dt[:].rearrange("p (b h) -> p b h", b=B),
                                repeat(neg_A[:], B), ALU.mult).then_inc(dta_ready, 1)
                dve.wait_ge(csT_ready, t + 1)
                then_settle(V.tensor_copy(cs_part[:, 0, :], bank[:, 2, 0:P]))
                then_settle(V.tensor_tensor(cs_rest[:, 0, :], bank[:, 2, 0:P], cs_part[:, 0, :], ALU.subtract))
                then_settle(V.tensor_copy(cs_part[:, 1, :], cs_rest[:, 0, :]))
                V.tensor_tensor(cs_part[:, 2, :], cs_rest[:, 0, :], cs_part[:, 1, :], ALU.subtract).then_inc(parts_ready, 1)
                for j in (0, 2):
                    for k in range(TAPS):
                        for jj in (j, j + 1):
                            n = BLOCKS[jj]
                            taps = pre[:, n, :, k:k + P]
                            if k == 0:
                                dve.wait_ge(pre_ready, t * 4 + jj + 1)
                                s.add(V.tensor_scalar(conv[:, n, :, :], taps, conv_w[:, n, 0:1], conv_b[:, n:n + 1],
                                                      ALU.mult, ALU.add))
                            else:
                                if jj == j:
                                    s.settle()
                                ins = V.scalar_tensor_tensor(out=conv[:, n, :, :], in0=taps,
                                                             scalar=conv_w[:, n, k:k + 1], in1=conv[:, n, :, :],
                                                             op0=ALU.mult, op1=ALU.add)
                                if k < TAPS - 1:
                                    s.add(ins)
                                else:
                                    ins.then_inc(conv_ready, 1)
                V.tensor_copy(pre[:, :, :, 0:TAPS - 1], pre[:, :, :, P:P + TAPS - 1]).then_inc(halo_ready, 1)
                dve.wait_ge(decays_ready, t + 1)
                for b in range(B):
                    hs = slice(b * NH, (b + 1) * NH)
                    as_heads = lambda ap: ap.rearrange("p (h c) -> p h c", h=NH)
                    dve.wait_ge(rows_ready, t * B + b + 1)
                    then_settle(V.tensor_tensor(as_heads(x_dt[:, b % 2, :]),
                                                as_heads(rows[:, b % 2, 2:4, :].rearrange("p k s -> p (k s)")),
                                                spread(dt[:, hs], HP), ALU.mult))
                    V.tensor_tensor(as_heads(x_ds[:, b % 2, :]), as_heads(x_dt[:, b % 2, :]),
                                    spread(decays[:, 1, hs], HP), ALU.mult).then_inc(xds_ready, 1)
                    for q in range(8):
                        dve.wait_ge(seg_ready, t * 32 + b * 8 + q + 1)
                        dve.wait_ge(ydiag_ready, t * 32 + b * 8 + q + 1)
                        V.tensor_tensor(mix[:, q % 2, :, :], seg[:, q % 2, :].rearrange("p (h l) -> p h l", h=4),
                                        repeat(rows[:, b % 2, 0, :], 4), ALU.mult).then_inc(mix_ready, 1)
                    dve.wait_ge(yoff_ready, t * B + b + 1)
                    s.add(V.tensor_tensor(as_heads(state[:, b, :]), as_heads(state[:, b, :]),
                                          spread(decays[:, 2, hs], HP), ALU.mult))
                    dve.wait_ge(ydiag_ready, t * 32 + b * 8 + 8 + 2)
                    then_settle(V.tensor_tensor(as_heads(y_off[:]), as_heads(bank[:, 6 - 3 * (b % 2), DI:2 * DI]),
                                                spread(decays[:, 0, hs], HP), ALU.mult))
                    V.tensor_tensor(state[:, b, :], state[:, b, :], bank[:, 1 + b % 2, 0:DI], ALU.add)
                    V.tensor_tensor(y[:, b, :], y_off[:], bank[:, 6 - 3 * (b % 2), 0:DI], ALU.add).then_inc(y_ready, 1)
                    dve.wait_ge(y_ready, t * B + b + 1)
                    s.add(V.bn_stats(stats_y[:, b, :], y[:, b, :]))
                s.settle()
                dve.sem_inc(dve_turn, 1)
                for b in range(B):
                    last = V.bn_aggr(mean_y[:, b, :], stats_y[:, b, :])
                last.then_inc(ystat_ready, 1)
                dve.wait_ge(yr_ready, t + 1)
                for b in range(B):
                    last = V.tensor_scalar(y[:, b, :], y[:, b, :], mean_y[:, b, 0:1], rstd_y[:, b:b + 1],
                                           ALU.subtract, ALU.mult)
                    s.add(last)
                for b in range(B):
                    if b == 0:
                        s.settle()
                    V.tensor_tensor(y[:, b, :], y[:, b, :], z_gate[:, b, :], ALU.mult).then_inc(g_ready, 1)
                x1 = x_all[:].rearrange("p (b t) d -> p b t d", b=B)[:, :, t, :]
                dve.wait_ge(out_ready, t + 1)
                V.tensor_tensor(x1, x1, bank[:, 3, :].rearrange("p (b d) -> p b d", b=B), ALU.add).then_inc(x1_ready, 1)
                dve.wait_ge(x1_ready, t + 2)
                dve.sem_inc(dve_turn, 1)
                for b in range(B):
                    last = V.bn_stats(stats2[:, b, :], x_all[:, b * NT + t, :])
                then_settle(last)
                dve.sem_inc(dve_turn, 1)
                for b in range(B):
                    last = V.bn_aggr(mean2[:, b, :], stats2[:, b, :])
                last.then_inc(stat2_ready, 1)
                dve.wait_ge(r2_ready, t + 1)
                for b in range(B):
                    last = V.tensor_scalar(h2[:, b, :], x_all[:, b * NT + t, :], mean2[:, b, 0:1],
                                           rstd2[:, b:b + 1], ALU.subtract, ALU.mult)
                then_settle(last)
                then_settle(V.tensor_tensor(h2[:], h2[:], gate_rows[:, :, 2 * D:3 * D], ALU.mult))
                V.tensor_tensor(h2[:], h2[:], gate_rows[:, :, D:2 * D], ALU.add).then_inc(h2_ready, 1)
                dve.wait_ge(h2_ready, t + 1)
                s.add(V.tensor_copy(h2_all[:].rearrange("p (b t) d -> p b t d", b=B)[:, :, t, :], h2[:]))
                dve.wait_ge(rms_ready, t + 1)
                s.settle()
                for b in range(B):
                    last = V.tensor_scalar(h2[:, b, :], h2[:, b, :], rms[:, b:b + 1], None, ALU.mult)
                last.then_inc(n2_ready, 1)
                assert s.n == DVE_STEPS

        @block.tensor
        def _(pe):
            MM, TR = nc.tensor.matmul, nc.tensor.transpose
            pe.wait_ge(loaded, LOADED)
            pe.wait_ge(c_ready, 2)
            MM(bank[:, 6, 0:B], w_modT[:, 0:D], c_silu[:], start=True, stop=True)
            MM(bank[:, 6, B:2 * B], w_modT[:, D:2 * D], c_silu[:], start=True, stop=True)
            for b in range(B):
                last = MM(bank[:, b, :], xn[:, b, :], w_modT[:, 2 * D:6 * D], start=True, stop=True)
            last.then_inc(mod_ready, 1)
            pe.wait_ge(mod_read, 2)
            pe.sem_inc(xnT_ready, 1)
            pe.sem_inc(ydiag_ready, 2)
            with pe.Fori(0, NT) as t:
                for b in range(B):
                    pe.wait_ge(xn_ready, t * B + b + 1)
                    last = TR(bank[:, 0, b * P:(b + 1) * P], xn[:, b, :], ident[:])
                last.then_inc(xnT_ready, 1)
                pe.wait_ge(hT_ready, t + 1)
                pe.wait_ge(x1_ready, t + 1)
                for b in range(B):
                    last = MM(bank[:, 3, b * NH:(b + 1) * NH], hT[:, b, :], w_in[:, DT0:PROJ], start=True, stop=True)
                last.then_inc(dtraw_ready, 1)
                for j in range(4):
                    n = BLOCKS[j]
                    if j >= 2:
                        pe.wait_ge(pre_ready, t * 4 + j - 1)
                    MM(bank[:, 1 + j % 2, :], w_in[:, XBC0 + n * P:XBC0 + (n + 1) * P],
                       hT[:].rearrange("p b s -> p (b s)"), start=True, stop=True).then_inc(xbc_ready, 1)
                for b in range(B):
                    if b == 2:
                        pe.wait_ge(v_ready, t + 1)
                    last = MM(bank[:, 3 * (b // 2), (b % 2) * DI:(b % 2 + 1) * DI], hT[:, b, :], w_in[:, Z0:Z0 + DI],
                              start=True, stop=True)
                    if b % 2:
                        last.then_inc(z_ready, 1)
                pe.wait_ge(dta_ready, t + 1)
                pe.wait_ge(pre_ready, t * 4 + 4)
                MM(bank[:, 2, 0:P], dta[:], tri[:, 0, :], start=True, stop=True).then_inc(csT_ready, 1)
                for k in range(3):
                    last = MM(bank[:, 1, k * P:(k + 1) * P], tri[:, k, :], dta[:], start=True, stop=True)
                last.then_inc(sums_ready, 1)
                pe.wait_ge(zgate_ready, t * 2 + 2)
                pe.wait_ge(xc_ready, t * 4 + 4)
                pe.wait_ge(seg_built, 16 * 15 * (t + 1))
                for b in range(B):
                    turned = 7 - 7 * (b % 2)
                    out = 6 - 3 * (b % 2)
                    if b >= 2:
                        pe.wait_ge(rows_ready, t * B + b - 1)
                        pe.wait_ge(y_ready, t * B + b - 1)
                    MM(bank[:, turned, 0:P], xc[:, 2, b, :], xc[:, 3, b, :], start=True, stop=True)
                    TR(bank[:, turned, P:2 * P], xc[:, 2, b, :], ident[:])
                    TR(bank[:, turned, 2 * P:3 * P], xc[:, 0, b, :], ident[:])
                    TR(bank[:, turned, 3 * P:4 * P], xc[:, 1, b, :], ident[:]).then_inc(turned_ready, 1)

                    def difference(q):
                        if q >= 2 or b > 0:
                            pe.wait_ge(seg_ready, t * 32 + b * 8 + q - 1)
                        MM(bank[:, 4 + q % 2, :], seg_lhs[0:3 * NH + 3, b, :],
                           seg_rhs[0:3 * NH + 3, b, q * 512:(q + 1) * 512], start=True, stop=False)
                        MM(bank[:, 4 + q % 2, :], ident_h[:], repeat(neg_mask[:], 4), start=False,
                           stop=True).then_inc(diff_ready, 1)

                    def diagonal(q):
                        pe.wait_ge(mix_ready, t * 32 + b * 8 + q + 1 + 2)
                        for h in range(4):
                            c = (4 * q + h) * HP
                            last = MM(bank[:, out, c:c + HP], mix[:, q % 2, h, :], x_dt[:, b % 2, c:c + HP],
                                      start=True, stop=True)
                        last.then_inc(ydiag_ready, 1)

                    difference(0)
                    difference(1)
                    pe.wait_ge(xds_ready, t * B + b + 1)
                    MM(bank[:, out, DI:2 * DI], xc[:, 3, b, :], state[:, b, :], start=True, stop=True)
                    MM(bank[:, 1 + b % 2, 0:DI], rows[:, b % 2, 1, :], x_ds[:, b % 2, :],
                       start=True, stop=True).then_inc(yoff_ready, 1)
                    for q in range(8):
                        diagonal(q)
                        if q + 2 < 8:
                            difference(q + 2)
                for b in range(B):
                    pe.wait_ge(g_ready, t * B + b + 1)
                    turned = 7 - 7 * (b // 2)
                    for k in range(2):
                        last = TR(bank[:, turned, (2 * (b % 2) + k) * P:(2 * (b % 2) + k + 1) * P],
                                  y[:, b, k * P:(k + 1) * P], ident[:])
                    if b % 2:
                        last.then_inc(gT_ready, 1)
                for b in range(B):
                    if b % 2 == 0:
                        pe.wait_ge(yT_ready, t * 2 + b // 2 + 1)
                    for k in range(2):
                        last = MM(bank[:, 3, b * D:(b + 1) * D], yT[:, b, k, :], w_out_b[:, b, k, :],
                                  start=(k == 0), stop=(k == 1))
                last.then_inc(out_ready, 1)
                pe.wait_ge(n2_ready, t + 1)
                for b in range(B):
                    last = TR(bank[:, 7, b * P:(b + 1) * P], h2[:, b, :], ident[:])
                last.then_inc(n2T_ready, 1)
                pe.wait_ge(n2Ts_ready, t + 1)
                MM(bank[:, 1, :], w_qkv[:, 0, :], n2T[:].rearrange("p b s -> p (b s)"), start=True, stop=True)
                MM(bank[:, 2, :], w_qkv[:, 1, :], n2T[:].rearrange("p b s -> p (b s)"), start=True, stop=True)
                for b in range(B):
                    last = MM(bank[:, 6, b * D:(b + 1) * D], n2T[:, b, :], w_qkv[:, 2, :], start=True, stop=True)
                last.then_inc(qkv_ready, 1)


def attention(nc, keep, scratch):
    ctx = ExitStack()
    with ctx:
        def sb(name, shape, dt=F32):
            return ctx.enter_context(nc.sbuf_tensor(name, shape, dt))

        def sem(name):
            return ctx.enter_context(nc.semaphore(name))

        GROUPS = B * HG
        KT = NT
        PER = 4 * KT
        TILES_A = 2 * PER
        AHEAD = 16
        O_AT = 10
        STRIPS = TILES_A + 3
        RING = 3
        QUARTER = L // 4
        bank = ctx.enter_context(nc.psum_tensor("bank_c", [P, 8, 512], F32))
        attn, ident = keep["attn_all"], keep["ident"]

        ka = sb("ka", [P, 2, 2, L], BF16)
        qa = sb("qa", [P, 2, 4, L], BF16)
        qb = sb("qb", [P, 2, 2, L], BF16)
        kb = sb("kb", [P, 2, 4, L], BF16)
        v_in = sb("v_in", [P, 2, KT, 4, AD])
        v_pad = sb("v_pad", [P, 2, KT, 4, 32])
        probs = sb("probs", [P, RING, 4, L])
        row_max = sb("row_max", [P, 2, 2, PER])
        neg_max = sb("neg_max", [P, 2, PER])
        max_part = sb("max_part", [PER, 3, P], BF16)
        max_rest = sb("max_rest", [PER, P])
        o_sb = sb("o_sb", [P, L])
        inv = sb("inv", [P, 2, 16])

        a_loaded = [sem(f"a_loaded{i}") for i in range(2)]
        b_loaded = [sem(f"b_loaded{i}") for i in range(2)]
        v_loaded = [sem(f"v_loaded{i}") for i in range(2)]
        qa_zeroed = sem("qa_zeroed")
        kb_zeroed = sem("kb_zeroed")
        max_placed = sem("max_placed")
        ones_ready = sem("ones_ready")
        v_ready = sem("v_padded")
        strip_filled = sem("strip_filled")
        strip_read = sem("strip_read")
        maxT_wanted = sem("maxT_wanted")
        max_split = sem("max_split")
        scores_ready = sem("scores_ready")
        probs_ready = sem("probs_ready")
        pv_done = sem("pv_done")
        o_copied = sem("o_copied")
        inv_ready = sem("inv_ready")
        dve_order = sem("dve_order_c")
        sp_turn = sem("sp_turn_c")
        pool_turn = sem("pool_turn_c")

        q_d = scratch["q"].rearrange("b (g j i) d c s -> (b g) (i d c) j s", g=HG, j=2)
        k_d = scratch["k"].rearrange("b (g j i) d c s -> (b g) (i d c) j s", g=HG, j=2)
        q_one = scratch["q"].rearrange("b (g j i) d c s -> (b g) i (d c) j s", g=HG, j=2)
        k_one = scratch["k"].rearrange("b (g j i) d c s -> (b g) i (d c) j s", g=HG, j=2)
        v_d = scratch["v"].rearrange("b g p t (h d) -> (b g) p t h d", h=4)

        def plan(i, c):
            g = c if i is None else None
            if g == -1:
                strips = [("a", 0, j) for j in range(TILES_A)] + [("m", 0, 0)]
            else:
                strips = [("a", c + 1, j) for j in range(AHEAD, TILES_A)] + [("m", c + 1, 0)]
                if g == GROUPS - 1:
                    strips = []
                if g != 0:
                    strips[O_AT if strips else 0:O_AT if strips else 0] = [("o", c - 1, 0), ("o", c - 1, 1)]
            if g is None or g < GROUPS - 2:
                strips += [("a", c + 2, j) for j in range(AHEAD)]
            return strips

        LOOPS = (GROUPS - 4) // 2
        counts = {-1: 0, 0: TILES_A + 1 + AHEAD}
        counts[1] = counts[0] + STRIPS - 2
        for g in range(2, GROUPS + 1):
            counts[g] = counts[g - 1] + len(plan(None, g - 1))
        assert counts[3] - counts[1] == 2 * STRIPS

        def before(i, c):
            if i is None:
                return counts[c]
            return counts[1] + (2 * i + c - 1) * STRIPS

        def group(i, c):
            return c if i is None else 2 * i + c

        def slot_round(i, c):
            return c // 2 if i is None else i + c // 2

        def steps(engine, step):
            step(None, 0)
            with engine.Fori(0, LOOPS) as i:
                step(i, 1)
                step(i, 2)
            for g in range(GROUPS - 3, GROUPS):
                step(None, g)

        def strip_bank(n):
            return 4 + n % 2

        block = ctx.enter_context(nc.Block())

        @block.sync
        def _(sp):
            def load_a(i, c):
                sp.dma_start(ka[:, c % 2, :, :], k_d[group(i, c)]).then_inc(a_loaded[c % 2], 16)
                for odd in range(2):
                    sp.dma_start(qa[64 * odd:64 * odd + 64, c % 2, odd::2, :],
                                 q_one[group(i, c), odd]).then_inc(a_loaded[c % 2], 16)

            def load_b(i, c):
                sp.dma_start(qb[:, c % 2, :, :], q_d[group(i, c)]).then_inc(b_loaded[c % 2], 16)
                for odd in range(2):
                    sp.dma_start(kb[64 * odd:64 * odd + 64, c % 2, odd::2, :],
                                 k_one[group(i, c), odd]).then_inc(b_loaded[c % 2], 16)
                sp.dma_start(v_in[:, c % 2, :, :, :], v_d[group(i, c)]).then_inc(v_loaded[c % 2], 16)

            def place_max(i, c):
                sp.wait_ge(max_split, group(i, c) + 1)
                sp.wait_ge(b_loaded[c % 2], 48 * (slot_round(i, c) + 1))
                sp.sem_inc(sp_turn, 1)
                for h in range(4):
                    for k in range(3):
                        row = 64 * (h % 2) + STACK * k + MAX_ROW
                        sp.dma_start(qb[row:row + 1, c % 2, h // 2, :],
                                     max_part[KT * h:KT * (h + 1), k, :]).then_inc(max_placed, 16)

            sp.wait_ge(qa_zeroed, 2)
            load_a(None, 0)
            load_a(None, 1)
            sp.wait_ge(kb_zeroed, 2)
            load_b(None, 0)
            place_max(None, 0)

            def step(i, c):
                g = c if i is None else None
                if g is None or g + 2 < GROUPS:
                    sp.wait_ge(strip_read, before(i, c))
                    sp.sem_inc(sp_turn, 1)
                    load_a(i, c + 2)
                if g is None or g + 1 < GROUPS:
                    if g != 0:
                        sp.wait_ge(pv_done, KT * group(i, c))
                        sp.sem_inc(sp_turn, 1)
                    load_b(i, c + 1)
                    place_max(i, c + 1)

            steps(sp, step)
            sp.wait_ge(max_placed, 16 * 12 * GROUPS)

        @block.gpsimd
        def _(pool):
            for slot in range(2):
                nc.gpsimd.memset(kb[:, slot, :, :], 0.0).then_inc(kb_zeroed, 1)
            nc.gpsimd.memset(v_pad[:], 1.0).then_inc(ones_ready, 1)
            pool.wait_ge(ones_ready, 1)

            def pad(i, c):
                pool.wait_ge(v_loaded[c % 2], 16 * (slot_round(i, c) + 1))
                pool.sem_inc(pool_turn, 1)
                nc.gpsimd.tensor_copy(v_pad[:, c % 2, :, :, 0:AD], v_in[:, c % 2, :, :, :]).then_inc(v_ready, 1)

            def step(i, c):
                if i is None and c == GROUPS - 1:
                    return
                if i is not None or c > 0:
                    pool.wait_ge(pv_done, KT * group(i, c))
                    pool.sem_inc(pool_turn, 1)
                pad(i, c + 1)

            pad(None, 0)
            steps(pool, step)

        @block.scalar
        def _(act):
            def step(i, c):
                for n in range(PER):
                    kt, h = n // 4, n % 4
                    act.wait_ge(scores_ready, group(i, c) * PER + n + 1)
                    used = kt - (1 if kt < KT % RING else RING - 1)
                    if i is not None or group(i, c) * KT + used > 0:
                        act.wait_ge(pv_done, group(i, c) * KT + used)
                    nc.scalar.activation(probs[:, kt % RING, h, :],
                                         bank[:, 2 * (n % 2):2 * (n % 2) + 2, :].rearrange("p a s -> p (a s)"),
                                         ACT.Exp).then_inc(probs_ready, 1)
                    if n == 4 and (i is not None or c > 0):
                        copy_o(i, c - 1)

            def copy_o(i, c):
                act.wait_ge(pv_done, KT * (group(i, c) + 1))
                nc.scalar.copy(o_sb[:], bank[:, 6:8, :].rearrange("p a s -> p (a s)")).then_inc(o_copied, 1)

            steps(act, step)
            copy_o(None, GROUPS - 1)

        @block.tensor
        def _(pe):
            MM, TR = nc.tensor.matmul, nc.tensor.transpose

            def fill(i, c, n, strip, wait):
                kind, of, j = strip
                if wait is not None:
                    pe.wait_ge(strip_read, wait)
                to = bank[:, strip_bank(n), :]
                if kind == "a":
                    if j in (0, AHEAD):
                        pe.wait_ge(a_loaded[of % 2], 48 * (slot_round(i, of) + 1))
                    h, qt, half = j // (2 * KT), j // 2 % KT, j % 2
                    last = MM(to, qa[:, of % 2, h, qt * P:(qt + 1) * P],
                              ka[:, of % 2, h // 2, half * 512:(half + 1) * 512], start=True, stop=True)
                elif kind == "m":
                    pe.wait_ge(maxT_wanted, group(i, of) + 1)
                    last = TR(to[0:PER, 0:P], neg_max[:, of % 2, :], ident[:])
                else:
                    pe.wait_ge(o_copied, group(i, of) + 1)
                    for k in range(4):
                        last = TR(to[:, k * P:(k + 1) * P], o_sb[:, (4 * j + k) * P:(4 * j + k + 1) * P], ident[:])
                last.then_inc(strip_filled, 1)

            def fills(i, c):
                base, out = before(i, c), []
                for n, strip in enumerate(plan(i, c)):
                    if i is None and c == -1 and n < 2:
                        need = None
                    else:
                        need = base + n - (1 if n else 0)
                    out.append((i, c, n, strip, need))
                return out

            def scores(i, c, n):
                kt, h = n // 4, n % 4
                if n == 0:
                    pe.wait_ge(b_loaded[c % 2], 48 * (slot_round(i, c) + 1))
                    pe.wait_ge(max_placed, 16 * 12 * (group(i, c) + 1))
                if i is not None or c > 0 or n >= 2:
                    pe.wait_ge(probs_ready, group(i, c) * PER + n - 1)
                for half in range(2):
                    last = MM(bank[:, 2 * (n % 2) + half, :], kb[:, c % 2, h, kt * P:(kt + 1) * P],
                              qb[:, c % 2, h // 2, half * 512:(half + 1) * 512], start=True, stop=True)
                last.then_inc(scores_ready, 1)

            def with_v(i, c, kt, quarter):
                if quarter == 0:
                    pe.wait_ge(probs_ready, group(i, c) * PER + 4 * kt + 4)
                if kt == 0 and quarter == 0:
                    pe.wait_ge(v_ready, group(i, c) + 1)
                    if i is not None or c > 0:
                        pe.wait_ge(o_copied, group(i, c))
                for h in range(4):
                    at = quarter % 2 * QUARTER
                    last = MM(bank[32 * h:32 * h + 32, 6 + quarter // 2, at:at + QUARTER], v_pad[:, c % 2, kt, h, :],
                              probs[:, kt % RING, h, quarter * QUARTER:(quarter + 1) * QUARTER],
                              start=(kt == 0 and quarter % 2 == 0), stop=(kt == KT - 1 and quarter % 2 == 1))
                if quarter == 3:
                    last.then_inc(pv_done, 1)

            for f in fills(None, -1):
                fill(*f)

            def step(i, c):
                todo = fills(i, c)
                g = c if i is None else None

                def fill_to(end, n):
                    while todo and todo[0][2] < end and not (todo[0][3][0] == "o" and n < 5):
                        fill(*todo.pop(0))

                for n in range(PER):
                    scores(i, c, n)
                    fill_to((2 * n + 1) * STRIPS // (2 * PER), n)
                    if n >= 5:
                        with_v(i, c, (n - 5) // 4, (n - 5) % 4)
                    elif g != 0:
                        with_v(i, c - 1, (n - 5) // 4 + KT, (n - 5) % 4)
                    fill_to((n + 1) * STRIPS // PER, n)
                assert not todo

            steps(pe, step)
            for n in range(5):
                with_v(None, GROUPS - 1, (n - 5) // 4 + KT, (n - 5) % 4)
            n = len(plan(None, GROUPS - 1))
            for half in range(2):
                fill(None, GROUPS - 1, half, ("o", GROUPS - 1, half), counts[GROUPS])

        @block.vector
        def _(dve):
            V = nc.vector

            def read(i, c, n, strip, at):
                kind, of, j = strip
                slot = of % 2
                dve.wait_ge(strip_filled, at + n + 1)
                frm = bank[:, strip_bank(n), :]
                if kind == "a":
                    V.tensor_reduce(row_max[:, slot, j % 2, j // 2:j // 2 + 1], frm, AXX, ALU.max).then_inc(strip_read, 1)
                elif kind == "m":
                    parts, rest = max_part, max_rest
                    order = 3 * group(i, of)
                    if i is not None or of > 0:
                        dve.wait_ge(max_placed, 16 * 12 * group(i, of))
                    V.tensor_copy(parts[:, 0, :], frm[0:PER, 0:P]).then_inc(dve_order, 1)
                    dve.wait_ge(dve_order, order + 2)
                    V.tensor_tensor(rest[:], frm[0:PER, 0:P], parts[:, 0, :], ALU.subtract).then_inc(strip_read, 1)
                    dve.wait_ge(strip_read, at + n + 1)
                    V.tensor_copy(parts[:, 1, :], rest[:]).then_inc(dve_order, 1)
                    dve.wait_ge(dve_order, order + 3)
                    V.tensor_tensor(parts[:, 2, :], rest[:], parts[:, 1, :], ALU.subtract).then_inc(max_split, 1)
                else:
                    outs = frm.rearrange("p (t h e) -> p t h e", t=4, h=4)
                    V.reciprocal(inv[:, j, :].rearrange("p (t h) -> p t h", t=4), outs[:, :, :, AD]).then_inc(inv_ready, 1)
                    dve.wait_ge(inv_ready, 2 * group(i, of) + j + 1)
                    g = group(i, of)
                    V.tensor_tensor(attn_g[:, bass.ds(g * KT * 4 * AD + j * 4 * 4 * AD, 4 * 4 * AD)]
                                    .rearrange("p (t h d) -> p t h d", t=4, h=4),
                                    outs[:, :, :, 0:AD],
                                    inv[:, j, :].rearrange("p (t h) -> p t h", t=4).unsqueeze(3)
                                    .to_broadcast([P, 4, 4, AD]), ALU.mult).then_inc(strip_read, 1)

            def combine(i, of, at, n):
                dve.wait_ge(strip_read, at + n)
                V.tensor_tensor(neg_max[:, of % 2, :], row_max[:, of % 2, 0, :], row_max[:, of % 2, 1, :],
                                ALU.max).then_inc(dve_order, 1)
                dve.wait_ge(dve_order, 3 * group(i, of) + 1)
                V.tensor_scalar(neg_max[:, of % 2, :], neg_max[:, of % 2, :], -1.0, None, ALU.mult).then_inc(maxT_wanted, 1)

            def step(i, c):
                at = before(i, c)
                strips = plan(i, c)
                for n, strip in enumerate(strips):
                    if strip[0] == "m":
                        combine(i, strip[1], at, n)
                    read(i, c, n, strip, at)

            attn_g = attn[:].rearrange("p n d -> p (n d)")
            for slot in range(2):
                V.memset(qa[:, slot, :, :], 0.0).then_inc(qa_zeroed, 1)
            step(None, -1)
            steps(dve, step)
            for half in range(2):
                read(None, GROUPS - 1, half, ("o", GROUPS - 1, half), counts[GROUPS])


def experts_and_out(nc, w, keep, out):
    ctx = ExitStack()
    with ctx:
        def sb(name, shape, dt=F32):
            return ctx.enter_context(nc.sbuf_tensor(name, shape, dt))

        def sem(name):
            return ctx.enter_context(nc.semaphore(name))

        bank = ctx.enter_context(nc.psum_tensor("bank_d", [P, 8, 512], F32))
        x1_all = keep["x_all"][:].rearrange("p (b t) d -> p b t d", b=B)
        h2_all = keep["h2_all"][:].rearrange("p (b t) d -> p b t d", b=B)
        attn = keep["attn_all"][:].rearrange("p n d -> p (n d)").rearrange("p (b g t c) -> p b g t c", b=B, g=HG, t=NT)
        gate_rows, ident = keep["gate_rows"], keep["ident"]
        KB = FF // P
        AT = (0, 1, 3, 4)

        w1 = sb("w1", [P, NE, FF])
        w3 = sb("w3", [P, NE, FF])
        w2 = sb("w2", [P, NE, KB, D])
        wo = sb("wo", [P, D])
        router = sb("router", [P, NE])
        rms2_col = sb("rms2_col", [P, 1])
        eps = sb("eps_d", [P, 1])
        expert_no = sb("expert_no", [P, NE])
        a_rows = sb("a_rows", [P, B, D])
        aT = sb("aT", [P, B, P])
        h3_next = sb("h3_next", [P, B, D])
        squares = sb("squares_d", [P, B, D])
        sumsq = sb("sumsq_d", [P, B])
        rms = sb("rms_d", [P, B])
        n3 = sb("n3", [P, B, D])
        n3T_next = sb("n3T_next", [P, B, P])
        n3T = sb("n3T", [P, B, P])
        logits = sb("logits", [P, B, NE])
        top = sb("top", [P, B, 8])
        top_at = sb("top_at", [P, B, 8], U32)
        top_no = sb("top_no", [P, B, 2])
        gap = sb("gap", [P, B])
        second = sb("second", [P, B])
        first_w = sb("first_w", [P, B])
        second_w = sb("second_w", [P, B])
        share1 = sb("share1", [P, B, NE])
        share_next = sb("share_next", [P, B, NE])
        share = sb("share", [P, B, NE])
        silu = sb("silu", [P, 2, B * P])
        hidden = sb("hidden", [P, 2, KB, B * P])
        acc = sb("acc", [P, B, D])
        result = sb("result", [P, B, D])

        w_loaded = sem("w_loaded")
        attn_taken = sem("attn_taken")
        aT_ready = sem("aT_ready")
        aT_copied = sem("aT_copied")
        o_ready = sem("o_ready")
        h3_ready = sem("h3_ready")
        rms_ready = sem("rms3_ready")
        n3_ready = sem("n3_ready")
        n3T_ready = sem("n3T_ready")
        next_ready = sem("next_ready")
        logits_ready = sem("logits_ready")
        gap_ready = sem("gap_ready")
        eps_ready = sem("eps_ready")
        gated = sem("gated")
        second_ready = sem("second_ready")
        share_ready = sem("share_ready")
        n3T_set = sem("n3T_set")
        acc_set = sem("acc_set")
        up_ready = sem("up_ready")
        silu_ready = sem("silu_ready")
        hidden_ready = sem("hidden_ready")
        down_ready = sem("down_ready")
        added = sem("added")
        result_ready = sem("result_ready")
        stored = sem("stored")
        dve_order = sem("dve_order_d")
        act_order = sem("act_order_d")
        sp_turn = sem("sp_turn_d")
        dve_turn = sem("dve_turn_d")

        loads = [(wo[:], w["wo_T"]), (rms2_col[:], w["ln2_col"]), (router[:], w["gate_w_T"]),
                 (expert_no[:], w["expert_no"].partition_broadcast(P)),
                 (w1[:], w["w1_T"]), (w3[:], w["w3_T"]), (w2[:], w["w2_T"])]
        LOADED = 16 * len(loads)
        out_rows = out.rearrange("b (t p) d -> t p b d", p=P)

        def steps(engine, lead_up, main):
            for part in lead_up(0):
                part()
            with engine.Fori(0, NT - 1) as t:
                main(t, lead_up(t + 1))
            main(NT - 1, None)

        block = ctx.enter_context(nc.Block())

        @block.sync
        def _(sp):
            for dst, src in loads:
                sp.dma_start(dst, src).then_inc(w_loaded, 16)
            with sp.Fori(0, NT) as t:
                sp.wait_ge(result_ready, t + 1)
                sp.sem_inc(sp_turn, 1)
                sp.dma_start(out_rows[t], result[:]).then_inc(stored, 16)
            sp.wait_ge(stored, 16 * (NT + 1))

        @block.tensor
        def _(pe):
            MM, TR = nc.tensor.matmul, nc.tensor.transpose
            pe.wait_ge(w_loaded, LOADED)

            def lead_up(t):
                def turn_attention():
                    pe.wait_ge(attn_taken, t + 1)
                    for b in range(B):
                        last = TR(bank[:, 0, b * P:(b + 1) * P], a_rows[:, b, :], ident[:])
                    last.then_inc(aT_ready, 1)

                def project():
                    pe.wait_ge(aT_copied, t + 1)
                    for b in range(B):
                        last = MM(bank[:, 1, b * D:(b + 1) * D], aT[:, b, :], wo[:], start=True, stop=True)
                    last.then_inc(o_ready, 1)

                def turn_norm():
                    pe.wait_ge(n3_ready, t + 1)
                    for b in range(B):
                        last = TR(bank[:, 0, b * P:(b + 1) * P], n3[:, b, :], ident[:])
                    last.then_inc(n3T_ready, 1)

                def route():
                    pe.wait_ge(next_ready, t + 1)
                    for b in range(B):
                        last = MM(bank[:, 1, b * NE:(b + 1) * NE], n3T_next[:, b, :], router[:], start=True, stop=True)
                    last.then_inc(logits_ready, 1)

                return [turn_attention, project, turn_norm, route]

            def main(t, parts):
                def up(e):
                    for k in range(KB):
                        n = e * KB + k
                        pe.wait_ge(hidden_ready, t * NE * KB + n - 1 + 2)
                        for m, ws in enumerate((w1, w3)):
                            last = MM(bank[:, 2 + 2 * m + n % 2, :], ws[:, e, k * P:(k + 1) * P],
                                      n3T[:].rearrange("p b s -> p (b s)"), start=True, stop=True)
                            last.then_inc(up_ready, 1)

                def down(e):
                    pe.wait_ge(hidden_ready, t * NE * KB + (e + 1) * KB + 2)
                    pe.wait_ge(added, t * NE + e - 1 + 2)
                    for b in range(B):
                        for k in range(KB):
                            last = MM(bank[:, 6 + e % 2, b * D:(b + 1) * D], hidden[:, e % 2, k, b * P:(b + 1) * P],
                                      w2[:, e, k, :], start=(k == 0), stop=(k == KB - 1))
                    last.then_inc(down_ready, 1)

                pe.wait_ge(n3T_set, t + 1)
                for e in range(NE):
                    up(e)
                    if e:
                        down(e - 1)
                    if parts and e in AT:
                        parts[AT.index(e)]()
                down(NE - 1)

            steps(pe, lead_up, main)

        @block.scalar
        def _(act):
            A = nc.scalar.activation
            act.wait_ge(w_loaded, LOADED)

            def lead_up(t):
                def take_attention():
                    for b in range(B):
                        last = nc.scalar.copy(a_rows[:, b, :].rearrange("p (g c) -> p g c", g=HG), attn[:, b, :, t, :])
                    last.then_inc(attn_taken, 1)

                def copy_turned():
                    act.wait_ge(aT_ready, t + 1)
                    nc.scalar.copy(aT[:].rearrange("p b s -> p (b s)"), bank[:, 0, :]).then_inc(aT_copied, 1)

                def root():
                    act.wait_ge(h3_ready, t + 1)
                    for b in range(B):
                        last = A(squares[:, b, :], h3_next[:, b, :], ACT.Square, accum_out=sumsq[:, b:b + 1])
                    last.then_inc(act_order, 1)
                    act.wait_ge(act_order, t * 2 + 1)
                    A(rms[:], sumsq[:], ACT.Ln, scale=1.0 / D, bias=eps[:]).then_inc(act_order, 1)
                    act.wait_ge(act_order, t * 2 + 2)
                    A(rms[:], rms[:], ACT.Exp, scale=-0.5).then_inc(rms_ready, 1)

                def scale_turned():
                    act.wait_ge(n3T_ready, t + 1)
                    A(n3T_next[:].rearrange("p b s -> p (b s)"), bank[:, 0, :], ACT.Copy,
                      scale=rms2_col[:, 0:1]).then_inc(next_ready, 1)

                def exp_gap():
                    act.wait_ge(gap_ready, t + 1)
                    A(second[:], gap[:], ACT.Exp).then_inc(second_ready, 1)

                return [take_attention, copy_turned, root, scale_turned, exp_gap]

            def main(t, parts):
                act.wait_ge(next_ready, t + 1)
                act.wait_ge(silu_ready, t * NE * KB + 1)
                nc.scalar.copy(n3T[:], n3T_next[:]).then_inc(n3T_set, 1)
                if parts:
                    parts[0]()
                for e in range(NE):
                    for k in range(KB):
                        n = e * KB + k
                        act.wait_ge(up_ready, 2 * (t * NE * KB + n + 1))
                        act.wait_ge(hidden_ready, t * NE * KB + n - 1 + 2)
                        A(silu[:, n % 2, :], bank[:, 2 + n % 2, :], ACT.Silu).then_inc(silu_ready, 1)
                    if parts and e in (0, 2, 3, 5):
                        parts[{0: 1, 2: 2, 3: 3, 5: 4}[e]]()

            act.sem_inc(silu_ready, 1)
            act.wait_ge(eps_ready, 1)
            steps(act, lead_up, main)

        @block.vector
        def _(dve):
            V = nc.vector
            V.memset(eps[:], RMS_EPS).then_inc(eps_ready, 1)
            dve.sem_inc(hidden_ready, 2)
            dve.sem_inc(added, 2)
            dve.wait_ge(w_loaded, LOADED)
            LEAD_STEPS = 8

            def lead_up(t):
                s = Steps(dve, dve_order, t * LEAD_STEPS)

                def then_settle(instruction):
                    s.add(instruction)
                    s.settle()

                def residual():
                    dve.wait_ge(o_ready, t + 1)
                    V.tensor_tensor(h3_next[:], h2_all[:, :, t, :],
                                    bank[:, 1, :].rearrange("p (b d) -> p b d", b=B), ALU.add).then_inc(h3_ready, 1)

                def norm():
                    dve.wait_ge(rms_ready, t + 1)
                    for b in range(B):
                        last = V.tensor_scalar(n3[:, b, :], h3_next[:, b, :], rms[:, b:b + 1], None, ALU.mult)
                    last.then_inc(n3_ready, 1)

                def top_two():
                    dve.wait_ge(logits_ready, t + 1)
                    then_settle(V.tensor_copy(logits[:], bank[:, 1, 0:B * NE].rearrange("p (b e) -> p b e", b=B)))
                    dve.sem_inc(dve_turn, 1)
                    for b in range(B):
                        last = V.max(top[:, b, :], logits[:, b, :])
                    then_settle(last)
                    dve.sem_inc(dve_turn, 1)
                    V.tensor_tensor(gap[:], top[:, :, 1], top[:, :, 0], ALU.subtract).then_inc(gap_ready, 1)
                    for b in range(B):
                        last = V.max_index(top_at[:, b, :], top[:, b, :], logits[:, b, :])
                    then_settle(last)
                    then_settle(V.tensor_copy(top_no[:], top_at[:, :, 0:2]))

                def shares():
                    dve.wait_ge(second_ready, t + 1)
                    then_settle(V.tensor_scalar(first_w[:], second[:], 1.0, None, ALU.add))
                    then_settle(V.reciprocal(first_w[:], first_w[:]))
                    then_settle(V.tensor_tensor(second_w[:], second[:], first_w[:], ALU.mult))
                    for b in range(B):
                        V.tensor_scalar(share1[:, b, :], expert_no[:], top_no[:, b, 0:1], first_w[:, b:b + 1],
                                        ALU.is_equal, ALU.mult)
                        last = V.tensor_scalar(share_next[:, b, :], expert_no[:], top_no[:, b, 1:2],
                                               second_w[:, b:b + 1], ALU.is_equal, ALU.mult)
                    then_settle(last)
                    V.tensor_tensor(share_next[:], share_next[:], share1[:], ALU.add).then_inc(share_ready, 1)
                    assert s.n == LEAD_STEPS, s.n

                return [residual, norm, top_two, shares]

            def main(t, parts):
                dve.wait_ge(share_ready, t + 1)
                dve.wait_ge(added, (t + 1) * NE + 2 - NE)
                V.tensor_copy(acc[:], h3_next[:])
                V.tensor_copy(share[:], share_next[:]).then_inc(acc_set, 1)
                dve.wait_ge(acc_set, t + 1)

                def add(e):
                    dve.wait_ge(down_ready, t * NE + e + 1)
                    if e:
                        dve.wait_ge(added, t * NE + e + 2)
                    for b in range(B):
                        last = V.scalar_tensor_tensor(out=acc[:, b, :], in0=bank[:, 6 + e % 2, b * D:(b + 1) * D],
                                                      scalar=share[:, b, e:e + 1], in1=acc[:, b, :],
                                                      op0=ALU.mult, op1=ALU.add)
                    last.then_inc(added, 1)

                for e in range(NE):
                    for k in range(KB):
                        n = e * KB + k
                        dve.wait_ge(silu_ready, t * NE * KB + n + 1 + 1)
                        V.tensor_tensor(hidden[:, e % 2, k, :], silu[:, n % 2, :], bank[:, 4 + n % 2, :],
                                        ALU.mult).then_inc(hidden_ready, 1)
                    if e:
                        add(e - 1)
                    if parts and e in (1, 2, 5, 6):
                        parts[{1: 0, 2: 1, 5: 2, 6: 3}[e]]()
                add(NE - 1)
                dve.wait_ge(added, (t + 1) * NE + 2)
                dve.wait_ge(stored, 16 * t + 16)
                V.tensor_tensor(result[:], acc[:], gate_rows[:, :, 3 * D:4 * D], ALU.mult).then_inc(gated, 1)
                dve.wait_ge(gated, t + 1)
                V.tensor_tensor(result[:], result[:], x1_all[:, :, t, :], ALU.add).then_inc(result_ready, 1)

            dve.sem_inc(stored, 16)
            steps(dve, lead_up, main)


def program(nc, w, out):
    with ExitStack() as ctx:
        def sb(name, shape, dt=F32):
            return ctx.enter_context(nc.sbuf_tensor(name, shape, dt))

        keep = {
            "x_all": sb("x_all", [P, TILES, D]),
            "h2_all": sb("h2_all", [P, TILES, D]),
            "attn_all": sb("attn_all", [P, TILES, D]),
            "gate_rows": sb("gate_rows", [P, B, 4 * D]),
            "ident": sb("ident", [P, P]),
        }
        scratch = {
            "q": nc.dram_tensor("q_stack", (B, AH, AD, STACK, L), BF16, kind="Internal").ap(),
            "k": nc.dram_tensor("k_stack", (B, AH, AD, STACK, L), BF16, kind="Internal").ap(),
            "v": nc.dram_tensor("v_groups", (B, HG, P, NT, 4 * AD), F32, kind="Internal").ap(),
        }
        state_space_and_qkv(nc, w, keep, scratch)
        attention(nc, keep, scratch)
        experts_and_out(nc, w, keep, out)


def kernel(**inputs):
    import ml_dtypes as _ml
    import numpy as _np
    import concourse.bacc as _bacc
    from concourse import mybir as _mybir
    from concourse.bass_utils import run_bass_kernel_spmd as _run

    bf16 = _np.dtype(_ml.bfloat16)
    laid = {}

    def put(name, a):
        laid[name] = _np.ascontiguousarray(a)

    put("u", inputs["L0_attn_u"])
    put("c_T", _np.asarray(inputs["L0_c"]).T)
    put("wmod", inputs["L0_wmod"])
    put("in_proj_T", _np.asarray(inputs["L0_attn_in_proj_w"]).T)
    put("out_proj_T", _np.asarray(inputs["L0_attn_out_proj_w"]).T)
    for name in ("conv_w", "dt_bias", "A_log"):
        put(name, inputs["L0_attn_" + name])
    put("conv_b_cols", _np.asarray(inputs["L0_attn_conv_b"]).reshape(4, P).T)
    put("ln_w_cols", _np.asarray(inputs["L0_attn_ln_w"]).reshape(2, P).T)
    put("ln1_col", _np.asarray(inputs["L0_ffn_ln1_w"]).reshape(P, 1))
    put("ln2_col", _np.asarray(inputs["L0_ffn_ln2_w"]).reshape(P, 1))
    for name in ("wq", "wk", "wv", "wo", "gate_w"):
        put(name + "_T", _np.asarray(inputs["L0_ffn_" + name]).T)
    put("w1_T", _np.asarray(inputs["L0_ffn_w1"]).transpose(2, 0, 1))
    put("w3_T", _np.asarray(inputs["L0_ffn_w3"]).transpose(2, 0, 1))
    put("w2_T", _np.asarray(inputs["L0_ffn_w2"]).reshape(NE, D, FF // P, P).transpose(3, 0, 2, 1))

    at = _np.arange(P)
    put("ident", _np.eye(P, dtype=_np.float32))
    put("ident_h", _np.eye(P, dtype=bf16))
    put("tri", _np.stack([at[:, None] <= at[None], at[:, None] > at[None],
                          _np.ones((P, P), bool)]).astype(_np.float32))
    put("neg_mask", _np.where(at[None] < at[:, None], -3e38, 0.0).astype(bf16))
    put("ones_h", _np.ones((3, B * P), bf16))
    put("expert_no", _np.arange(NE, dtype=_np.float32))
    put("neg_delta", _np.tile(_np.repeat(-_np.eye(NH), P, axis=1), (3, 1)).astype(bf16))
    pad = _np.zeros((AH, AD, STACK - MAX_ROW, L), bf16)
    put("q_pad", pad.reshape(P, STACK - MAX_ROW, L))
    pad = pad.copy()
    pad[:, 0:3, 0] = 1
    put("k_pad", pad.reshape(P, STACK - MAX_ROW, L))

    nc = _bacc.Bacc("TRN2", target_bir_lowering=False, num_devices=1)
    w = {k: nc.dram_tensor(f"in_{k}", a.shape, _mybir.dt.from_np(a.dtype), kind="ExternalInput").ap()
         for k, a in laid.items()}
    out = nc.dram_tensor("out_x", (B, L, D), F32, kind="ExternalOutput").ap()
    program(nc, w, out)
    r = _run(nc, [{f"in_{k}": a for k, a in laid.items()}], core_ids=[0])
    return r.results[0]["out_x"]
```

```python
from contextlib import ExitStack

import concourse.bass as bass
from concourse import mybir

F32 = mybir.dt.float32
BF16 = mybir.dt.bfloat16
U32 = mybir.dt.uint32
ALU = mybir.AluOpType
ACT = mybir.ActivationFunctionType
AXX = mybir.AxisListType.X

P = 128
B, L, D = 4, 1024, 128
NT = L // P
TILES = B * NT
NH, HP, DI, DS = 32, 8, 256, 128
PROJ = 2 * DI + 2 * DS + NH
TAPS = 4
AH, AD = 16, 8
HG = AH // 4
NE, FF = 8, 256
LN_EPS, RMS_EPS = 1e-5, 1e-5
GATE_MIN = 0.25
SCALE = float(AD) ** -0.5
LN_EXP_SET = "natural_log_exp_and_others"

Z0, XBC0, DT0 = 0, DI, 2 * DI + 2 * DS
BLOCKS = (2, 3, 0, 1)
Q_PART = (0, 1, 0, 2, 0, 1)
K_PART = (0, 0, 1, 0, 2, 1)
STACK = 8
MAX_ROW = 6


class Steps:

    def __init__(self, engine, order, base):
        self.engine, self.order, self.base, self.n = engine, order, base, 0

    def add(self, instruction):
        self.n += 1
        instruction.then_inc(self.order, 1)

    def settle(self):
        self.engine.wait_ge(self.order, self.base + self.n)


def spread(ap, n):
    return ap.unsqueeze(2).to_broadcast([ap.shape[0], ap.shape[1], n])


def repeat(ap, n):
    return ap.unsqueeze(1).to_broadcast([ap.shape[0], n, ap.shape[1]])


def state_space_and_qkv(nc, w, keep, scratch):
    ctx = ExitStack()
    with ctx:
        def sb(name, shape, dt=F32):
            return ctx.enter_context(nc.sbuf_tensor(name, shape, dt))

        def sem(name):
            return ctx.enter_context(nc.semaphore(name))

        NQ = B * NH // 4
        PER_B = NH // 4
        RING = 4
        TURN_AT, ROWS_AT, INPUTS_AT = 4, 5, 6
        STATE_AT, SCALE_AT, YOFF_AT, ADD_AT = 5, 6, 6, 7
        COPY_AT, BACK_AT, Y_AT, STATS_AT = 2, 3, 4, 5

        def wait(engine, semaphore, value):
            if not isinstance(value, int) or value > 0:
                engine.wait_ge(semaphore, value)

        def run(engine, core, tail, lead):
            def step(t, v, u):
                for k in range(NQ):
                    if core:
                        core(t, k)
                    for at, part in tail:
                        if at == k and v is not None:
                            part(v)
                    for at, part in lead:
                        if at == k and u is not None:
                            part(u)

            for _, part in sorted(lead, key=lambda entry: entry[0]):
                part(0)
            step(0, None, 1)
            step(1, 0, 2)
            with engine.Fori(0, NT - 3) as i:
                step(i + 2, i + 1, i + 3)
            step(NT - 1, NT - 2, None)
            for _, part in sorted(tail, key=lambda entry: entry[0]):
                part(NT - 1)

        bank = ctx.enter_context(nc.psum_tensor("bank_a", [P, 8, 512], F32))
        x_all, h2_all = keep["x_all"], keep["h2_all"]
        gate_rows = keep["gate_rows"]
        ident = keep["ident"]

        w_in = sb("w_in", [P, PROJ])
        w_out = sb("w_out", [P, 2, D])
        w_out_b = sb("w_out_b", [P, B, 2, D])
        w_qkv = sb("w_qkv", [P, 3, D])
        w_modT = sb("w_modT", [P, 6 * D])
        c_col = sb("c_col", [P, B])
        c_silu = sb("c_silu", [P, B])
        scale1 = sb("scale1", [P, B])
        shift1 = sb("shift1", [P, B])
        ln_w_col = sb("ln_w_col", [P, 2])
        rms1_col = sb("rms1_col", [P, 1])
        conv_w = sb("conv_w", [P, 4, TAPS])
        conv_b = sb("conv_b", [P, 4])
        dt_bias = sb("dt_bias", [P, NH])
        neg_A = sb("neg_A", [P, NH])
        eps_col = sb("eps_col", [P, 1])
        tri = sb("tri", [P, 3, P])
        ident_h = sb("ident_h", [P, P], BF16)
        neg_mask = sb("neg_mask", [P, P], BF16)
        gate_sign = sb("gate_sign", [P, B, D])

        stats1 = sb("stats1", [P, TILES, 6])
        mean1 = sb("mean1", [P, TILES, 2])
        rstd1 = sb("rstd1", [P, TILES])
        xn = sb("xn", [P, B, D])
        hT = sb("hT", [P, B, P])
        dt_v = sb("dt_v", [P, B * NH])
        dt_abs = sb("dt_abs", [P, B * NH])
        dt_u = sb("dt_u", [P, B * NH])
        dt_w = sb("dt_w", [P, B * NH])
        dt_ln = sb("dt_ln", [P, B * NH])
        dt_c = sb("dt_c", [P, B * NH])
        dt_r = sb("dt_r", [P, B * NH])
        dt = sb("dt", [P, B * NH])
        dta = sb("dta", [P, B * NH])
        decays_new = sb("decays_new", [P, 3, B * NH])
        decays = sb("decays", [P, 2, B * NH])
        dt_now = sb("dt_now", [P, B * NH])
        dt_end = sb("dt_end", [P, B * NH])
        cs_part = sb("cs_part", [P, 3, P], BF16)
        cs_rest = sb("cs_rest", [P, P])
        seg_lhs = sb("seg_lhs", [P, B, P], BF16)
        seg_rhs = sb("seg_rhs", [P, B, NH * P], BF16)
        pre = sb("pre", [P, 4, B, TAPS - 1 + P])
        conv = sb("conv", [P, 4, B, P])
        xc = sb("xc", [P, 4, B, P])
        z_new = sb("z_new", [P, B, DI])
        z_gate = sb("z_gate", [P, B, DI])
        rows = sb("rows", [P, 2, 4, P])
        x_pad = sb("x_pad", [P, 2, NH // 4, 4 * 40])
        x_ds = sb("x_ds", [P, 2, DI])
        seg = sb("seg", [P, RING, 4 * P])
        mix = sb("mix", [P, RING, 4, P])
        y_rowsT = sb("y_rowsT", [P, DI])
        state = sb("state", [P, B, DI])
        y_off = sb("y_off", [P, DI])
        y = sb("y", [P, B, DI])
        stats_y = sb("stats_y", [P, B, 6])
        mean_y = sb("mean_y", [P, B, 2])
        rstd_y = sb("rstd_y", [P, B])
        yT = sb("yT", [P, B, 2, P])
        stats2 = sb("stats2", [P, B, 6])
        mean2 = sb("mean2", [P, B, 2])
        rstd2 = sb("rstd2", [P, B])
        h2 = sb("h2", [P, B, D])
        squares = sb("squares", [P, B, D])
        sumsq = sb("sumsq", [P, B])
        rms = sb("rms", [P, B])
        n2T = sb("n2T", [P, B, P])
        qk = sb("qk", [P, 2, B * P])
        qk_part = sb("qk_part", [P, 3, 2, B * P], BF16)
        qk_rest = sb("qk_rest", [P, 2, B * P])
        v_rows = sb("v_rows", [P, B, D])

        mod_loaded = sem("mod_loaded")
        loaded = sem("loaded")
        seg_loaded = sem("seg_loaded")
        x_loaded = sem("x_loaded")
        dve_order = sem("dve_order_a")
        act_order = sem("act_order_a")
        pool_order = sem("pool_order_a")
        sp_turn = sem("sp_turn_a")
        dve_turn = sem("dve_turn_a")
        zeroed = sem("zeroed")
        c_ready = sem("c_ready")
        mod_ready = sem("mod_ready")
        mod_read = sem("mod_read")
        gates_ready = sem("gates_ready")
        stats1_ready = sem("stats1_ready")
        rstd1_ready = sem("rstd1_ready")
        negA_ready = sem("negA_ready")
        xn_ready = sem("xn_ready")
        xnT_ready = sem("xnT_ready")
        hT_ready = sem("hT_ready")
        dtraw_ready = sem("dtraw_ready")
        v_ready = sem("v_ready")
        u_ready = sem("u_ready")
        w_ready = sem("w_ready")
        ln_ready = sem("ln_ready")
        dta_ready = sem("dta_ready")
        xbc_ready = sem("xbc_ready")
        pre_ready = sem("pre_ready")
        halo_ready = sem("halo_ready")
        z_ready = sem("z_ready")
        conv_ready = sem("conv_ready")
        xc_ready = sem("xc_ready")
        sums_ready = sem("sums_ready")
        csT_ready = sem("csT_ready")
        decays_ready = sem("decays_ready")
        parts_ready = sem("parts_ready")
        seg_built = [sem(f"seg_built{b}") for b in range(B)]
        xdt_ready = sem("xdt_ready")
        yT_copied = sem("yT_copied")
        yback_ready = sem("yback_ready")
        decays_copied = sem("decays_copied")
        z_new_ready = sem("z_new_ready")
        z_kept = sem("z_kept")
        z_copied = sem("z_copied")
        part0_ready = sem("part0_ready")
        part1_ready = sem("part1_ready")
        rest_ready = sem("rest_ready")
        tail_order = sem("tail_order")
        lead_order = sem("lead_order")
        tap_done = sem("tap_done")
        qk_ready = sem("qk_ready")
        vrow_ready = sem("vrow_ready")
        pad_zeroed = sem("pad_zeroed")
        dt_now_ready = sem("dt_now_ready")
        state_scaled = sem("state_scaled")
        y_off_ready = sem("y_off_ready")
        product_ready = sem("product_ready")
        state_ready = sem("state_ready")
        h2n_ready = sem("h2n_ready")
        h2_kept = sem("h2_kept")
        y_stats_ready = sem("y_stats_ready")
        yn_ready = sem("yn_ready")
        x1_stats = sem("x1_stats")
        turned_ready = sem("turned_ready")
        rows_ready = sem("rows_ready")
        xds_ready = sem("xds_ready")
        diff_ready = sem("diff_ready")
        seg_ready = sem("seg_ready")
        mix_ready = sem("mix_ready")
        ydiag_ready = sem("ydiag_ready")
        yoff_ready = sem("yoff_ready")
        y_ready = sem("y_ready")
        ystat_ready = sem("ystat_ready")
        yr_ready = sem("yr_ready")
        g_ready = sem("g_ready")
        gT_ready = sem("gT_ready")
        yT_ready = sem("yT_ready")
        out_ready = sem("out_ready")
        stat2_ready = sem("stat2_ready")
        r2_ready = sem("r2_ready")
        h2_ready = sem("h2_ready")
        rms_ready = sem("rms_ready")
        n2_ready = sem("n2_ready")
        n2T_ready = sem("n2T_ready")
        n2Ts_ready = sem("n2Ts_ready")
        v_copied = sem("v_copied")
        x1_ready = sem("x1_ready")
        pool_turn = sem("pool_turn_a")
        qk_copied = sem("qk_copied")
        split_ready = sem("split_ready")
        qk_stored = sem("qk_stored")
        v_stored = sem("v_stored")
        pads_stored = sem("pads_stored")

        xd = w["u"].rearrange("b (t p) d -> p (b t) d", p=P)
        q_stack = scratch["q"].rearrange("b h d c s -> (h d) b c s")
        k_stack = scratch["k"].rearrange("b h d c s -> (h d) b c s")
        v_scr = scratch["v"].rearrange("b g p t c -> p b g t c")
        mod_loads = [(c_col[:], w["c_T"]), (w_modT[:], w["wmod"])]
        loads = [
            (w_in[:], w["in_proj_T"]), (w_out[:], w["out_proj_T"].rearrange("(k p) n -> p k n", p=P)),
            (w_qkv[:, 0, :], w["wq_T"]), (w_qkv[:, 1, :], w["wk_T"]), (w_qkv[:, 2, :], w["wv_T"]),
            (ln_w_col[:], w["ln_w_cols"]),
            (rms1_col[:], w["ln1_col"]),
            (conv_w[:], w["conv_w"].rearrange("(k p) j -> p k j", p=P)),
            (conv_b[:], w["conv_b_cols"]),
            (dt_bias[:], w["dt_bias"].partition_broadcast(P)), (neg_A[:], w["A_log"].partition_broadcast(P)),
            (ident[:], w["ident"]), (ident_h[:], w["ident_h"]), (neg_mask[:], w["neg_mask"]),
            (tri[:], w["tri"].rearrange("k p n -> p k n")),
        ]
        seg_loads = [
            (seg_lhs[3 * NH:3 * NH + 3, :, :], w["ones_h"].rearrange("k (b s) -> k b s", b=B)),
        ] + [(seg_rhs[0:3 * NH, b, :], w["neg_delta"]) for b in range(B)]
        MOD_LOADED, LOADED, SEG_LOADED = 16 * len(mod_loads), 16 * len(loads), 16 * len(seg_loads)

        block = ctx.enter_context(nc.Block())

        @block.sync
        def _(sp):
            for dst, src in mod_loads:
                sp.dma_start(dst, src).then_inc(mod_loaded, 16)
            for b in range(B):
                sp.dma_start(x_all[:, b * NT:(b + 1) * NT, :], xd[:, b * NT:(b + 1) * NT, :]).then_inc(x_loaded, 16)
            for dst, src in loads:
                sp.dma_start(dst, src).then_inc(loaded, 16)
            for dst, src in seg_loads:
                sp.dma_start(dst, src).then_inc(seg_loaded, 16)
            for b in range(B):
                sp.dma_start(q_stack[:, b, MAX_ROW:, :], w["q_pad"]).then_inc(pads_stored, 16)
                sp.dma_start(k_stack[:, b, MAX_ROW:, :], w["k_pad"]).then_inc(pads_stored, 16)

            def build_segments(u, b):
                wait(sp, diff_ready, NQ * u - NQ + PER_B * (b + 1))
                sp.sem_inc(sp_turn, 1)
                sp.wait_ge(parts_ready, u + 1)
                sp.sem_inc(sp_turn, 1)
                for k in range(3):
                    heads = cs_part[NH * b:NH * (b + 1), k, :]
                    sp.dma_start(seg_rhs[3 * NH + k:3 * NH + k + 1, b, :], heads).then_inc(seg_built[b], 16)
                    sp.dma_start(seg_lhs[NH * k:NH * (k + 1), b, :], heads).then_inc(seg_built[b], 16)

            def store_qkv(v):
                sp.wait_ge(split_ready, v + 1)
                sp.sem_inc(sp_turn, 1)
                tokens = bass.ds(v * P, P)
                for c in range(MAX_ROW):
                    sp.dma_start(q_stack[:, :, c, tokens],
                                 qk_part[:, Q_PART[c], 0, :].rearrange("p (b s) -> p b s", b=B)).then_inc(qk_stored, 16)
                    sp.dma_start(k_stack[:, :, c, tokens],
                                 qk_part[:, K_PART[c], 1, :].rearrange("p (b s) -> p b s", b=B)).then_inc(qk_stored, 16)
                sp.wait_ge(v_copied, v + 1)
                sp.sem_inc(sp_turn, 1)
                sp.dma_start(v_scr[:, :, :, v, :],
                             v_rows[:].rearrange("p b (g c) -> p b g c", g=HG)).then_inc(v_stored, 16)

            run(sp, None,
                [(31, store_qkv)],
                [(13, lambda u: build_segments(u, 0)), (15, lambda u: build_segments(u, 1)),
                 (22, lambda u: build_segments(u, 2)), (30, lambda u: build_segments(u, 3))])
            sp.wait_ge(qk_stored, 16 * 2 * MAX_ROW * NT)
            sp.wait_ge(v_stored, 16 * NT)
            sp.wait_ge(pads_stored, 16 * 2 * B)

        @block.scalar
        def _(act):
            A = nc.scalar.activation
            act.wait_ge(mod_loaded, MOD_LOADED)
            A(c_silu[:], c_col[:], ACT.Silu).then_inc(c_ready, 1)
            nc.scalar.preload_act_table_set(LN_EXP_SET)
            act.wait_ge(loaded, LOADED)
            A(neg_A[:], neg_A[:], ACT.Exp).then_inc(act_order, 1)
            act.wait_ge(act_order, 1)
            nc.scalar.mul(neg_A[:], neg_A[:], -1.0).then_inc(negA_ready, 1)
            act.wait_ge(zeroed, 1)
            act.wait_ge(stats1_ready, 1)
            A(rstd1[:], mean1[:, :, 1], ACT.Ln, bias=eps_col[:]).then_inc(act_order, 1)
            act.wait_ge(act_order, 2)
            A(rstd1[:], rstd1[:], ACT.Exp, scale=-0.5).then_inc(rstd1_ready, 1)
            act.wait_ge(mod_read, 1)
            act.wait_ge(loaded, LOADED)

            def exponential(t, k):
                act.wait_ge(diff_ready, NQ * t + k + 1)
                wait(act, mix_ready, NQ * t + k + 1 - RING)
                A(seg[:, k % RING, :], bank[:, 4 + k % 2, :], ACT.Exp).then_inc(seg_ready, 1)

            def copy_rows(t, b):
                act.wait_ge(turned_ready, B * t + b + 1)
                wait(act, mix_ready, NQ * t + PER_B * (b - 1))
                wait(act, xds_ready, B * t + b - 1)
                nc.scalar.copy(rows[:, b % 2, :, :],
                               bank[:, 7, :].rearrange("p (k s) -> p k s", k=4)).then_inc(rows_ready, 1)

            def copy_yT(t, b):
                act.wait_ge(ydiag_ready, NQ * t + PER_B * (b + 1))
                wait(act, yback_ready, B * t + b)
                nc.scalar.copy(y_rowsT[:], bank[:, 3, 0:DI]).then_inc(yT_copied, 1)

            def core(t, k):
                if k == 30 or (k == 0 and isinstance(t, int) and t == 0):
                    nc.scalar.preload_act_table_set(LN_EXP_SET)
                exponential(t, k)
                if k % PER_B == ROWS_AT and k // PER_B + 1 < B:
                    copy_rows(t, k // PER_B + 1)
                if k % PER_B == COPY_AT and k > PER_B:
                    copy_yT(t, k // PER_B - 1)

            def modulate(u):
                act.wait_ge(xnT_ready, u + 1)
                for b in range(B):
                    last = A(hT[:, b, :], bank[:, 0, b * P:(b + 1) * P], ACT.Identity,
                             scale=scale1[:, b:b + 1], bias=shift1[:, b:b + 1])
                last.then_inc(hT_ready, 1)

            def softplus_exp(u):
                act.wait_ge(v_ready, u + 1)
                A(dt_u[:], dt_abs[:], ACT.Exp, scale=-1.0).then_inc(u_ready, 1)

            def softplus_ln(u):
                act.wait_ge(w_ready, u + 1)
                A(dt_ln[:], dt_w[:], ACT.Ln).then_inc(ln_ready, 1)

            def decay(u):
                act.wait_ge(sums_ready, u + 1)
                wait(act, decays_copied, u)
                A(decays_new[:].rearrange("p k c -> p (k c)"), bank[:, 1, 0:3 * P], ACT.Exp).then_inc(decays_ready, 1)

            def channels(j):
                def copy(u):
                    wait(act, halo_ready, u)
                    act.wait_ge(xbc_ready, 4 * u + j + 1)
                    nc.scalar.copy(pre[:, BLOCKS[j], :, TAPS - 1:],
                                   bank[:, j % 2, :].rearrange("p (b s) -> p b s", b=B)).then_inc(pre_ready, 1)
                return copy

            def keep_z(k):
                def copy(u):
                    wait(act, z_copied, u)
                    act.wait_ge(z_ready, 2 * u + k + 1)
                    nc.scalar.copy(z_new[:, 2 * k:2 * k + 2, :], bank[:, 1 - k, :]).then_inc(z_kept, 1)
                return copy

            def silus(u):
                act.wait_ge(z_kept, 2 * u + 2)
                A(z_new[:], z_new[:], ACT.Silu).then_inc(z_new_ready, 1)
                wait(act, yoff_ready, B * u)
                for j in range(4):
                    act.wait_ge(conv_ready, 4 * u + j + 1)
                    A(xc[:, BLOCKS[j], :, :], conv[:, BLOCKS[j], :, :], ACT.Silu).then_inc(xc_ready, 1)

            def rstd_of_y(v):
                act.wait_ge(ystat_ready, v + 1)
                A(rstd_y[:], mean_y[:, :, 1], ACT.Ln, bias=eps_col[:]).then_inc(tail_order, 1)
                act.wait_ge(tail_order, 4 * v + 1)
                A(rstd_y[:], rstd_y[:], ACT.Exp, scale=-0.5).then_inc(yr_ready, 1)

            def copy_gT(k):
                def copy(v):
                    act.wait_ge(gT_ready, 2 * v + k + 1)
                    nc.scalar.copy(yT[:, 2 * k:2 * k + 2, :, :].rearrange("p b k s -> p (b k s)"),
                                   bank[:, k, :]).then_inc(yT_ready, 1)
                return copy

            def rstd_of_h2(v):
                act.wait_ge(stat2_ready, v + 1)
                A(rstd2[:], mean2[:, :, 1], ACT.Ln, bias=eps_col[:]).then_inc(tail_order, 1)
                act.wait_ge(tail_order, 4 * v + 2)
                A(rstd2[:], rstd2[:], ACT.Exp, scale=-0.5).then_inc(r2_ready, 1)

            def rms_of_h2(v):
                act.wait_ge(h2_ready, v + 1)
                for b in range(B):
                    last = A(squares[:, b, :], h2[:, b, :], ACT.Square, accum_out=sumsq[:, b:b + 1])
                last.then_inc(tail_order, 1)
                act.wait_ge(tail_order, 4 * v + 3)
                A(rms[:], sumsq[:], ACT.Ln, scale=1.0 / D, bias=eps_col[:]).then_inc(tail_order, 1)
                act.wait_ge(tail_order, 4 * v + 4)
                A(rms[:], rms[:], ACT.Exp, scale=-0.5).then_inc(rms_ready, 1)

            def copy_n2T(v):
                act.wait_ge(n2T_ready, v + 1)
                A(n2T[:].rearrange("p b s -> p (b s)"), bank[:, 1, :], ACT.Copy,
                  scale=rms1_col[:, 0:1]).then_inc(n2Ts_ready, 1)

            def copy_q(v):
                wait(act, split_ready, v)
                wait(act, qk_stored, 16 * 2 * MAX_ROW * v)
                act.wait_ge(qk_ready, 2 * v + 1)
                nc.scalar.mul(qk[:, 0, :], bank[:, 0, :], SCALE).then_inc(qk_copied, 1)

            def copy_k(v):
                act.wait_ge(qk_ready, 2 * v + 2)
                nc.scalar.copy(qk[:, 1, :], bank[:, 1, :]).then_inc(qk_copied, 1)
                act.wait_ge(qk_copied, 2 * v + 2)
                nc.scalar.copy(qk_part[:, 0, :, :], qk[:]).then_inc(part0_ready, 1)

            def second_part(v):
                act.wait_ge(rest_ready, v + 1)
                nc.scalar.copy(qk_part[:, 1, :, :], qk_rest[:]).then_inc(part1_ready, 1)

            def copy_v(v):
                wait(act, v_stored, 16 * v)
                act.wait_ge(vrow_ready, v + 1)
                nc.scalar.copy(v_rows[:].rearrange("p b c -> p (b c)"), bank[:, 0, :]).then_inc(v_copied, 1)

            run(act, core,
                [(1, lambda v: copy_yT(v, B - 1)), (5, rstd_of_y), (10, copy_gT(0)), (12, copy_gT(1)), (17, rstd_of_h2),
                 (22, rms_of_h2), (24, copy_n2T), (27, copy_q), (27, copy_k), (28, copy_v), (30, second_part)],
                [(4, modulate), (6, softplus_exp), (6, channels(0)), (7, channels(1)), (8, softplus_ln),
                 (8, channels(2)), (9, channels(3)), (14, decay), (15, keep_z(0)), (17, keep_z(1)), (29, silus),
                 (31, lambda u: copy_rows(u, 0))])

        @block.gpsimd
        def _(pool):
            G = nc.gpsimd
            G.memset(x_pad[:], 0.0).then_inc(pad_zeroed, 1)
            pool.wait_ge(pad_zeroed, 1)

            def inputs_by_dt(t, b):
                pool.wait_ge(rows_ready, B * t + b + 1)
                pool.wait_ge(dt_now_ready, 2 * t + 2)
                wait(pool, ydiag_ready, NQ * t + PER_B * (b - 1))
                hs = slice(b * NH, (b + 1) * NH)
                x_rows = rows[:, b % 2, 2:4, :].rearrange("p k (h c) -> p (k h) c", c=HP)
                G.tensor_tensor(x_pad[:, b % 2, :, :].rearrange("p n (r e) -> p (n r) e", r=4)[:, :, 0:HP], x_rows,
                                spread(dt_now[:, hs], HP), ALU.mult).then_inc(xdt_ready, 1)
                G.tensor_tensor(x_ds[:, b % 2, :].rearrange("p (h c) -> p h c", h=NH), x_rows,
                                spread(dt_end[:, hs], HP), ALU.mult).then_inc(xds_ready, 1)

            def scale_state(t, b):
                pool.wait_ge(yoff_ready, B * t + b + 1)
                pool.wait_ge(decays_copied, t + 1)
                as_heads = state[:, b, :].rearrange("p (h c) -> p h c", h=NH)
                G.tensor_tensor(as_heads, as_heads, spread(decays[:, 1, b * NH:(b + 1) * NH], HP),
                                ALU.mult).then_inc(state_scaled, 1)

            def core(t, k):
                b = k // PER_B
                if k % PER_B == INPUTS_AT and b + 1 < B:
                    inputs_by_dt(t, b + 1)
                if k % PER_B == SCALE_AT:
                    scale_state(t, b)
                if k == 8:
                    take_z(t)

            def take_z(u):
                pool.wait_ge(z_new_ready, u + 1)
                wait(pool, g_ready, B * u)
                pool.sem_inc(pool_turn, 1)
                G.tensor_copy(z_gate[:], z_new[:]).then_inc(z_copied, 1)

            def take_dt(u):
                pool.wait_ge(dta_ready, u + 1)
                pool.wait_ge(decays_ready, u + 1)
                wait(pool, xdt_ready, B * u)
                wait(pool, xds_ready, B * u)
                G.tensor_tensor(dt_end[:], dt[:], decays_new[:, 1, :], ALU.mult).then_inc(dt_now_ready, 1)
                pool.sem_inc(pool_turn, 1)
                G.tensor_copy(dt_now[:], dt[:]).then_inc(dt_now_ready, 1)

            def take_decays(u):
                wait(pool, y_off_ready, B * u)
                wait(pool, state_scaled, B * u)
                pool.sem_inc(pool_turn, 1)
                G.tensor_copy(decays[:], decays_new[:, 0::2, :]).then_inc(decays_copied, 1)

            def modulate_h2(v):
                pool.wait_ge(gates_ready, 1)
                pool.wait_ge(h2n_ready, v + 1)
                G.tensor_tensor(h2[:], h2[:], gate_rows[:, :, 2 * D:3 * D], ALU.mult).then_inc(pool_order, 1)
                pool.wait_ge(pool_order, v + 1)
                G.tensor_tensor(h2[:], h2[:], gate_rows[:, :, D:2 * D], ALU.add).then_inc(h2_ready, 1)
                pool.wait_ge(h2_ready, v + 1)
                pool.sem_inc(pool_turn, 1)
                G.tensor_copy(h2_all[:].rearrange("p (b t) d -> p b t d", b=B)[:, :, v, :], h2[:]).then_inc(h2_kept, 1)

            def first_rest(v):
                pool.wait_ge(part0_ready, v + 1)
                G.tensor_tensor(qk_rest[:], qk[:], qk_part[:, 0, :, :], ALU.subtract).then_inc(rest_ready, 1)

            def second_rest(v):
                pool.wait_ge(part1_ready, v + 1)
                G.tensor_tensor(qk_part[:, 2, :, :], qk_rest[:], qk_part[:, 1, :, :], ALU.subtract).then_inc(split_ready, 1)

            run(pool, core,
                [(18, modulate_h2), (28, first_rest), (31, second_rest)],
                [(28, take_dt), (30, lambda u: inputs_by_dt(u, 0)), (31, take_decays)])

        @block.vector
        def _(dve):
            V = nc.vector
            V.memset(eps_col[:], LN_EPS)
            V.memset(pre[:, :, :, 0:TAPS - 1], 0.0)
            V.memset(state[:], 0.0).then_inc(zeroed, 1)
            dve.wait_ge(c_ready, 1)
            for b in range(B):
                last = V.tensor_copy(xn[:, b, :], c_silu[:, b:b + 1].to_broadcast([P, P]))
            last.then_inc(c_ready, 1)
            dve.wait_ge(x_loaded, 16 * B)
            for i in range(TILES):
                last = V.bn_stats(stats1[:, i, :], x_all[:, i, :])
            last.then_inc(dve_order, 1)
            dve.wait_ge(dve_order, 1)
            for i in range(TILES):
                last = V.bn_aggr(mean1[:, i, :], stats1[:, i, :])
            last.then_inc(stats1_ready, 1)
            dve.wait_ge(mod_ready, 1)
            V.tensor_copy(shift1[:], bank[:, 6, 0:B])
            V.tensor_scalar(scale1[:], bank[:, 6, B:2 * B], 1.0, None, ALU.add)
            for b in range(B):
                last = V.tensor_copy(gate_rows[:, b, :], bank[:, b, :])
            last.then_inc(mod_read, 1)
            dve.wait_ge(rstd1_ready, 1)
            dve.wait_ge(negA_ready, 1)

            def as_heads(ap):
                return ap.rearrange("p (h c) -> p h c", h=NH)

            def mix_heads(t, k):
                b = k // PER_B
                if k % PER_B == 0:
                    dve.wait_ge(rows_ready, B * t + b + 1)
                dve.wait_ge(seg_ready, NQ * t + k + 1)
                wait(dve, ydiag_ready, NQ * t + k + 1 - RING)
                V.tensor_tensor(mix[:, k % RING, :, :], seg[:, k % RING, :].rearrange("p (h l) -> p h l", h=4),
                                repeat(rows[:, b % 2, 0, :], 4), ALU.mult).then_inc(mix_ready, 1)

            def decay_y_off(t, b):
                dve.wait_ge(yoff_ready, B * t + b + 1)
                dve.wait_ge(decays_copied, t + 1)
                V.tensor_tensor(as_heads(y_off[:]), as_heads(bank[:, 6, DI:2 * DI]),
                                spread(decays[:, 0, b * NH:(b + 1) * NH], HP), ALU.mult).then_inc(y_off_ready, 1)

            def add_state(t, b):
                dve.wait_ge(product_ready, B * t + b + 1)
                dve.wait_ge(state_scaled, B * t + b + 1)
                V.tensor_tensor(state[:, b, :], state[:, b, :], bank[:, 2, 0:DI], ALU.add).then_inc(state_ready, 1)

            def add_y(t, b):
                dve.wait_ge(yback_ready, B * t + b + 1)
                if b == 0:
                    wait(dve, gT_ready, 2 * t)
                V.tensor_tensor(y[:, b, :], y_off[:], bank[:, 6, 0:DI], ALU.add).then_inc(y_ready, 1)

            def y_stats(t, b):
                dve.wait_ge(y_ready, B * t + b + 1)
                V.bn_stats(stats_y[:, b, :], y[:, b, :]).then_inc(y_stats_ready, 1)

            def core(t, k):
                b = k // PER_B
                mix_heads(t, k)
                if k % PER_B == YOFF_AT:
                    decay_y_off(t, b)
                if k % PER_B == ADD_AT:
                    add_state(t, b)
                if k % PER_B == Y_AT and b:
                    add_y(t, b - 1)
                if k % PER_B == STATS_AT and b:
                    y_stats(t, b - 1)

            def normalise_x(u):
                wait(dve, xnT_ready, u)
                for b in range(B):
                    i = b * NT + u
                    V.tensor_scalar(xn[:, b, :], x_all[:, i, :], mean1[:, i, 0:1], rstd1[:, bass.ds(i, 1)],
                                    ALU.subtract, ALU.mult).then_inc(xn_ready, 1)

            LEAD_STEPS = 9

            def dt_raw(u):
                s = Steps(dve, lead_order, u * LEAD_STEPS)
                dve.wait_ge(dtraw_ready, u + 1)
                s.add(V.tensor_tensor(dt_v[:].rearrange("p (b h) -> p b h", b=B),
                                      bank[:, 1, 0:P].rearrange("p (b h) -> p b h", b=B),
                                      repeat(dt_bias[:], B), ALU.add))
                s.settle()
                V.scalar_tensor_tensor(out=dt_abs[:], in0=dt_v[:], scalar=-1.0, in1=dt_v[:], op0=ALU.mult,
                                       op1=ALU.max).then_inc(v_ready, 1)

            def dt_sum(u):
                s = Steps(dve, lead_order, u * LEAD_STEPS + 1)
                dve.wait_ge(u_ready, u + 1)
                V.tensor_scalar(dt_w[:], dt_u[:], 1.0, None, ALU.add).then_inc(w_ready, 1)
                dve.wait_ge(w_ready, u + 1)
                s.add(V.reciprocal(dt_r[:], dt_w[:]))
                s.add(V.scalar_tensor_tensor(out=dt_c[:], in0=dt_w[:], scalar=-1.0, in1=dt_u[:],
                                             op0=ALU.add, op1=ALU.subtract))
                s.settle()
                s.add(V.tensor_tensor(dt_c[:], dt_c[:], dt_r[:], ALU.mult))

            def dt_last(u):
                s = Steps(dve, lead_order, u * LEAD_STEPS + 4)
                dve.wait_ge(ln_ready, u + 1)
                wait(dve, dt_now_ready, 2 * u)
                s.add(V.scalar_tensor_tensor(out=dt[:], in0=dt_v[:], scalar=0.0, in1=dt_ln[:],
                                             op0=ALU.max, op1=ALU.add))
                s.settle()
                s.add(V.tensor_tensor(dt[:], dt[:], dt_c[:], ALU.subtract))
                s.settle()
                V.tensor_tensor(dta[:].rearrange("p (b h) -> p b h", b=B), dt[:].rearrange("p (b h) -> p b h", b=B),
                                repeat(neg_A[:], B), ALU.mult).then_inc(dta_ready, 1)

            def split_sums(u):
                s = Steps(dve, lead_order, u * LEAD_STEPS + 6)
                dve.wait_ge(csT_ready, u + 1)
                for b in range(B):
                    wait(dve, seg_built[b], 16 * 6 * u)
                s.add(V.tensor_copy(cs_part[:, 0, :], bank[:, 0, 0:P]))
                s.settle()
                s.add(V.tensor_tensor(cs_rest[:], bank[:, 0, 0:P], cs_part[:, 0, :], ALU.subtract))
                s.settle()
                s.add(V.tensor_copy(cs_part[:, 1, :], cs_rest[:]))
                s.settle()
                V.tensor_tensor(cs_part[:, 2, :], cs_rest[:], cs_part[:, 1, :], ALU.subtract).then_inc(parts_ready, 1)

            def tap(j, k):
                def one(u):
                    for jj in (j, j + 1):
                        n = BLOCKS[jj]
                        taps = pre[:, n, :, k:k + P]
                        if k == 0:
                            dve.wait_ge(pre_ready, 4 * u + jj + 1)
                            wait(dve, xc_ready, 4 * u)
                            V.tensor_scalar(conv[:, n, :, :], taps, conv_w[:, n, 0:1], conv_b[:, n:n + 1],
                                            ALU.mult, ALU.add).then_inc(tap_done, 1)
                        else:
                            dve.wait_ge(tap_done, 12 * u + 6 * (j // 2) + 2 * (k - 1) + (jj - j) + 1)
                            V.scalar_tensor_tensor(out=conv[:, n, :, :], in0=taps, scalar=conv_w[:, n, k:k + 1],
                                                   in1=conv[:, n, :, :], op0=ALU.mult, op1=ALU.add
                                                   ).then_inc(tap_done if k < TAPS - 1 else conv_ready, 1)
                return one

            def make_gates(u):
                if not (isinstance(u, int) and u == 0):
                    return
                dve.wait_ge(mod_read, 1)
                V.tensor_scalar(gate_rows[:, :, 2 * D:3 * D], gate_rows[:, :, 2 * D:3 * D], 1.0, None, ALU.add)
                order = 1
                for g in (0, 3):
                    gate = gate_rows[:, :, g * D:(g + 1) * D]
                    V.tensor_scalar(gate_sign[:], gate, 0.0, 2.0, ALU.is_ge, ALU.mult).then_inc(dve_order, 1)
                    order += 1
                    dve.wait_ge(dve_order, order)
                    V.scalar_tensor_tensor(out=gate, in0=gate, scalar=-1.0, in1=gate, op0=ALU.mult,
                                           op1=ALU.max).then_inc(dve_order, 1)
                    order += 1
                    dve.wait_ge(dve_order, order)
                    V.tensor_scalar(gate, gate, GATE_MIN, None, ALU.max).then_inc(dve_order, 1)
                    order += 1
                    dve.wait_ge(dve_order, order)
                    V.scalar_tensor_tensor(out=gate, in0=gate_sign[:], scalar=-1.0, in1=gate, op0=ALU.add,
                                           op1=ALU.mult).then_inc(dve_order, 1)
                    order += 1
                    dve.wait_ge(dve_order, order)
                dve.wait_ge(loaded, LOADED)
                for b in range(B):
                    for k in range(2):
                        last = V.scalar_tensor_tensor(out=w_out_b[:, b, k, :], in0=w_out[:, k, :],
                                                      scalar=ln_w_col[:, k:k + 1], in1=gate_rows[:, b, 0:D],
                                                      op0=ALU.mult, op1=ALU.mult)
                last.then_inc(gates_ready, 1)

            def keep_halo(u):
                V.tensor_copy(pre[:, :, :, 0:TAPS - 1], pre[:, :, :, P:P + TAPS - 1]).then_inc(halo_ready, 1)

            def end_y(v):
                add_y(v, B - 1)

            def end_y_stats(v):
                y_stats(v, B - 1)
                dve.wait_ge(y_stats_ready, B * (v + 1))
                dve.sem_inc(dve_turn, 1)
                for b in range(B):
                    last = V.bn_aggr(mean_y[:, b, :], stats_y[:, b, :])
                last.then_inc(ystat_ready, 1)

            def normalise_y(v):
                dve.wait_ge(yr_ready, v + 1)
                for b in range(B):
                    V.tensor_scalar(y[:, b, :], y[:, b, :], mean_y[:, b, 0:1], rstd_y[:, b:b + 1],
                                    ALU.subtract, ALU.mult).then_inc(yn_ready, 1)

            def gate_y(v):
                dve.wait_ge(z_copied, v + 1)
                for b in range(B):
                    dve.wait_ge(yn_ready, B * v + b + 1)
                    V.tensor_tensor(y[:, b, :], y[:, b, :], z_gate[:, b, :], ALU.mult).then_inc(g_ready, 1)

            def add_output(v):
                x1 = x_all[:].rearrange("p (b t) d -> p b t d", b=B)[:, :, v, :]
                dve.wait_ge(out_ready, v + 1)
                V.tensor_tensor(x1, x1, bank[:, 0, :].rearrange("p (b d) -> p b d", b=B), ALU.add).then_inc(x1_ready, 1)
                dve.wait_ge(x1_ready, v + 1)
                dve.sem_inc(dve_turn, 1)
                for b in range(B):
                    last = V.bn_stats(stats2[:, b, :], x_all[:, b * NT + v, :])
                last.then_inc(x1_stats, 1)

            def h2_stats(v):
                dve.wait_ge(x1_stats, v + 1)
                dve.sem_inc(dve_turn, 1)
                for b in range(B):
                    last = V.bn_aggr(mean2[:, b, :], stats2[:, b, :])
                last.then_inc(stat2_ready, 1)

            def normalise_h2(v):
                dve.wait_ge(r2_ready, v + 1)
                wait(dve, n2T_ready, v)
                for b in range(B):
                    last = V.tensor_scalar(h2[:, b, :], x_all[:, b * NT + v, :], mean2[:, b, 0:1],
                                           rstd2[:, b:b + 1], ALU.subtract, ALU.mult)
                last.then_inc(h2n_ready, 1)

            def scale_h2(v):
                dve.wait_ge(rms_ready, v + 1)
                dve.wait_ge(h2_kept, v + 1)
                for b in range(B):
                    last = V.tensor_scalar(h2[:, b, :], h2[:, b, :], rms[:, b:b + 1], None, ALU.mult)
                last.then_inc(n2_ready, 1)

            run(dve, core,
                [(3, end_y), (4, end_y_stats), (6, normalise_y), (6, gate_y), (14, add_output), (15, h2_stats),
                 (18, normalise_h2), (22, scale_h2)],
                [(1, normalise_x), (5, dt_raw), (7, dt_sum), (8, tap(0, 0)), (9, dt_last), (10, tap(0, 1)),
                 (11, tap(0, 2)), (12, split_sums), (13, tap(0, 3)), (16, tap(2, 0)), (19, tap(2, 1)),
                 (22, tap(2, 2)), (24, tap(2, 3)), (25, keep_halo), (31, make_gates)])

        @block.tensor
        def _(pe):
            MM, TR = nc.tensor.matmul, nc.tensor.transpose
            pe.wait_ge(mod_loaded, MOD_LOADED)
            pe.wait_ge(c_ready, 2)
            MM(bank[:, 6, 0:B], w_modT[:, 0:D], c_silu[:], start=True, stop=True)
            MM(bank[:, 6, B:2 * B], w_modT[:, D:2 * D], c_silu[:], start=True, stop=True)
            for b in range(B):
                last = MM(bank[:, b, :], xn[:, b, :], w_modT[:, 2 * D:6 * D], start=True, stop=True)
            last.then_inc(mod_ready, 1)
            pe.wait_ge(mod_read, 1)
            pe.wait_ge(loaded, LOADED)

            def difference(t, k):
                b, q = k // PER_B, k % PER_B
                wait(pe, seg_ready, NQ * t + k - 1)
                if q == 0 and isinstance(t, int) and t == 0:
                    pe.wait_ge(seg_loaded, SEG_LOADED)
                if q == 0:
                    pe.wait_ge(seg_built[b], 16 * 6 * (t + 1))
                of_heads = seg_rhs[0:3 * NH + 3, b, :].rearrange("p (f j r l) -> p f r j l", f=2, j=4, r=4)
                MM(bank[:, 4 + k % 2, :], seg_lhs[0:3 * NH + 3, b, :], of_heads[:, q // 4, q % 4, :, :],
                   start=True, stop=False)
                MM(bank[:, 4 + k % 2, :], ident_h[:], repeat(neg_mask[:], 4), start=False,
                   stop=True).then_inc(diff_ready, 1)

            def diagonal(t, k):
                b, q = k // PER_B, k % PER_B
                if q == 0:
                    pe.wait_ge(xdt_ready, B * t + b + 1)
                    wait(pe, yT_copied, B * t + b)
                pe.wait_ge(mix_ready, NQ * t + k + 1)
                half, r = q // 4, q % 4
                for j in range(4):
                    last = MM(bank[32 * j:32 * j + 32, 3, half * P:(half + 1) * P],
                              x_pad[:, b % 2, 4 * half + j, 32 * r:32 * r + 32], mix[:, k % RING, j, :],
                              start=(r == 0), stop=(r == 3))
                last.then_inc(ydiag_ready, 1)

            def turn(t, b):
                pe.wait_ge(xc_ready, 4 * t + 4)
                wait(pe, rows_ready, B * t + b)
                MM(bank[:, 7, 0:P], xc[:, 2, b, :], xc[:, 3, b, :], start=True, stop=True)
                TR(bank[:, 7, P:2 * P], xc[:, 2, b, :], ident[:])
                TR(bank[:, 7, 2 * P:3 * P], xc[:, 0, b, :], ident[:])
                TR(bank[:, 7, 3 * P:4 * P], xc[:, 1, b, :], ident[:]).then_inc(turned_ready, 1)

            def use_state(t, b):
                wait(pe, y_ready, B * t + b)
                wait(pe, state_ready, B * t + b)
                MM(bank[:, 6, DI:2 * DI], xc[:, 3, b, :], state[:, b, :], start=True, stop=True).then_inc(yoff_ready, 1)
                pe.wait_ge(xds_ready, B * t + b + 1)
                MM(bank[:, 2, 0:DI], rows[:, b % 2, 1, :], x_ds[:, b % 2, :],
                   start=True, stop=True).then_inc(product_ready, 1)

            def turn_back(t, b):
                pe.wait_ge(yT_copied, B * t + b + 1)
                pe.wait_ge(y_off_ready, B * t + b + 1)
                for k in range(2):
                    last = TR(bank[:, 6, k * P:(k + 1) * P], y_rowsT[:, k * P:(k + 1) * P], ident[:])
                last.then_inc(yback_ready, 1)

            def core(t, k):
                if k + 2 < NQ:
                    difference(t, k + 2)
                if k:
                    diagonal(t, k - 1)
                b = k // PER_B
                if k % PER_B == TURN_AT and b + 1 < B:
                    turn(t, b + 1)
                if k % PER_B == STATE_AT:
                    use_state(t, b)
                if k % PER_B == BACK_AT and b:
                    turn_back(t, b - 1)

            def turn_xn(u):
                wait(pe, z_kept, 2 * u)
                wait(pe, v_copied, u - 2)
                for b in range(B):
                    pe.wait_ge(xn_ready, B * u + b + 1)
                    last = TR(bank[:, 0, b * P:(b + 1) * P], xn[:, b, :], ident[:])
                last.then_inc(xnT_ready, 1)

            def project_dt(u):
                pe.wait_ge(hT_ready, u + 1)
                wait(pe, qk_copied, 2 * u - 4)
                for b in range(B):
                    last = MM(bank[:, 1, b * NH:(b + 1) * NH], hT[:, b, :], w_in[:, DT0:PROJ], start=True, stop=True)
                last.then_inc(dtraw_ready, 1)

            def sum_to(u):
                pe.wait_ge(dta_ready, u + 1)
                pe.wait_ge(pre_ready, 4 * u + 3)
                wait(pe, yT_ready, 2 * u - 3)
                MM(bank[:, 0, 0:P], dta[:], tri[:, 0, :], start=True, stop=True).then_inc(csT_ready, 1)

            def sum_all(u):
                pe.wait_ge(pre_ready, 4 * u + 4)
                wait(pe, yT_ready, 2 * u - 2)
                for k in range(3):
                    last = MM(bank[:, 1, k * P:(k + 1) * P], tri[:, k, :], dta[:], start=True, stop=True)
                last.then_inc(sums_ready, 1)

            def project_channels(j):
                def project(u):
                    n = BLOCKS[j]
                    if j == 1:
                        pe.wait_ge(v_ready, u + 1)
                    if j >= 2:
                        pe.wait_ge(pre_ready, 4 * u + j - 1)
                    MM(bank[:, j % 2, :], w_in[:, XBC0 + n * P:XBC0 + (n + 1) * P],
                       hT[:].rearrange("p b s -> p (b s)"), start=True, stop=True).then_inc(xbc_ready, 1)
                return project

            def project_z(k):
                def project(u):
                    if k == 0:
                        pe.wait_ge(decays_ready, u + 1)
                    else:
                        pe.wait_ge(parts_ready, u + 1)
                        wait(pe, x1_ready, u - 1)
                    for n in range(2):
                        last = MM(bank[:, 1 - k, n * DI:(n + 1) * DI], hT[:, 2 * k + n, :], w_in[:, Z0:Z0 + DI],
                                  start=True, stop=True)
                    last.then_inc(z_ready, 1)
                return project

            def turn_g(k):
                def turn_half(v):
                    if isinstance(v, int) and v + 2 >= NT:
                        pe.wait_ge(v_copied, v)
                        pe.wait_ge(qk_copied, 2 * v)
                    else:
                        pe.wait_ge(pre_ready, 4 * v + 11 + k)
                    for b in (2 * k, 2 * k + 1):
                        pe.wait_ge(g_ready, B * v + b + 1)
                        for n in range(2):
                            last = TR(bank[:, k, (2 * (b % 2) + n) * P:(2 * (b % 2) + n + 1) * P],
                                      y[:, b, n * P:(n + 1) * P], ident[:])
                    last.then_inc(gT_ready, 1)
                return turn_half

            def project_out(v):
                pe.wait_ge(gates_ready, 1)
                if not isinstance(v, int) or v + 2 < NT:
                    pe.wait_ge(parts_ready, v + 3)
                for b in range(B):
                    if b % 2 == 0:
                        pe.wait_ge(yT_ready, 2 * v + b // 2 + 1)
                    for k in range(2):
                        last = MM(bank[:, 0, b * D:(b + 1) * D], yT[:, b, k, :], w_out_b[:, b, k, :],
                                  start=(k == 0), stop=(k == 1))
                last.then_inc(out_ready, 1)

            def turn_n2(v):
                pe.wait_ge(z_kept, 2 * NT if isinstance(v, int) and v + 2 >= NT else 2 * v + 6)
                pe.wait_ge(n2_ready, v + 1)
                for b in range(B):
                    last = TR(bank[:, 1, b * P:(b + 1) * P], h2[:, b, :], ident[:])
                last.then_inc(n2T_ready, 1)

            def project_qk(v):
                pe.wait_ge(n2Ts_ready, v + 1)
                for k in range(2):
                    MM(bank[:, k, :], w_qkv[:, k, :], n2T[:].rearrange("p b s -> p (b s)"),
                       start=True, stop=True).then_inc(qk_ready, 1)

            def project_v(v):
                pe.wait_ge(qk_copied, 2 * v + 1)
                for b in range(B):
                    last = MM(bank[:, 0, b * D:(b + 1) * D], n2T[:, b, :], w_qkv[:, 2, :], start=True, stop=True)
                last.then_inc(vrow_ready, 1)

            def end_diagonal(v):
                diagonal(v, NQ - 1)

            run(pe, core,
                [(0, end_diagonal), (2, lambda v: turn_back(v, B - 1)), (9, turn_g(0)), (10, turn_g(1)),
                 (13, project_out), (23, turn_n2), (25, project_qk), (27, project_v)],
                [(2, turn_xn), (4, project_dt), (5, project_channels(0)), (6, project_channels(1)),
                 (7, project_channels(2)), (8, project_channels(3)), (11, sum_to), (13, sum_all), (14, project_z(0)), (15, project_z(1)),
                 (30, lambda u: turn(u, 0)), (30, lambda u: difference(u, 0)), (31, lambda u: difference(u, 1))])


def attention(nc, w, keep, scratch):
    ctx = ExitStack()
    with ctx:
        def sb(name, shape, dt=F32):
            return ctx.enter_context(nc.sbuf_tensor(name, shape, dt))

        def sem(name):
            return ctx.enter_context(nc.semaphore(name))

        GROUPS = B * HG
        KT = NT
        PER = 4 * KT
        TILES_A = 2 * PER
        AHEAD = 20
        O_AT = 12
        STRIPS = TILES_A + 3
        RING = 3
        QUARTER = L // 4
        bank = ctx.enter_context(nc.psum_tensor("bank_c", [P, 8, 512], F32))
        attn, ident = keep["attn_all"], keep["ident"]

        ka = sb("ka", [P, 2, 2, L], BF16)
        qa = sb("qa", [P, 2, 4, L], BF16)
        qb = sb("qb", [P, 2, 2, L], BF16)
        kb = sb("kb", [P, 2, 4, L], BF16)
        v_in = sb("v_in", [P, 2, KT, 4, AD])
        v_pad = sb("v_pad", [P, 2, KT, 4, 32])
        probs = sb("probs", [P, RING, 4, L])
        row_max = sb("row_max", [P, 2, 2, PER])
        neg_max = sb("neg_max", [P, 2, PER])
        max_part = sb("max_part", [PER, 3, P], BF16)
        max_rest = sb("max_rest", [PER, P])
        o_sb = sb("o_sb", [P, L])
        inv = sb("inv", [P, 2, 16])

        a_loaded = [sem(f"a_loaded{i}") for i in range(2)]
        b_loaded = [sem(f"b_loaded{i}") for i in range(2)]
        v_loaded = [sem(f"v_loaded{i}") for i in range(2)]
        qa_zeroed = sem("qa_zeroed")
        kb_zeroed = sem("kb_zeroed")
        max_placed = sem("max_placed")
        ones_ready = sem("ones_ready")
        v_ready = sem("v_padded")
        experts_loaded = sem("experts_loaded")
        strip_filled = sem("strip_filled")
        strip_read = sem("strip_read")
        maxT_wanted = sem("maxT_wanted")
        max_split = sem("max_split")
        scores_ready = sem("scores_ready")
        probs_ready = sem("probs_ready")
        pv_done = sem("pv_done")
        first_half_done = sem("first_half_done")
        o_copied = sem("o_copied")
        inv_ready = sem("inv_ready")
        dve_order = sem("dve_order_c")
        sp_turn = sem("sp_turn_c")
        pool_turn = sem("pool_turn_c")

        q_d = scratch["q"].rearrange("b (g j i) d c s -> (b g) (i d c) j s", g=HG, j=2)
        k_d = scratch["k"].rearrange("b (g j i) d c s -> (b g) (i d c) j s", g=HG, j=2)
        q_one = scratch["q"].rearrange("b (g j i) d c s -> (b g) i (d c) j s", g=HG, j=2)
        k_one = scratch["k"].rearrange("b (g j i) d c s -> (b g) i (d c) j s", g=HG, j=2)
        v_d = scratch["v"].rearrange("b g p t (h d) -> (b g) p t h d", h=4)

        def plan(i, c):
            g = c if i is None else None
            if g == -1:
                strips = [("a", 0, j) for j in range(TILES_A)] + [("m", 0, 0)]
            else:
                strips = [("a", c + 1, j) for j in range(AHEAD, TILES_A)] + [("m", c + 1, 0)]
                if g == GROUPS - 1:
                    strips = []
                if g != 0:
                    strips[O_AT if strips else 0:O_AT if strips else 0] = [("o", c - 1, 0), ("o", c - 1, 1)]
            if g is None or g < GROUPS - 2:
                ahead = [("a", c + 2, j) for j in range(AHEAD)]
                strips = strips[:-1] + ahead[:2] + strips[-1:] + ahead[2:]
            return strips

        LOOPS = (GROUPS - 4) // 2
        counts = {-1: 0, 0: TILES_A + 1 + AHEAD}
        counts[1] = counts[0] + STRIPS - 2
        for g in range(2, GROUPS + 1):
            counts[g] = counts[g - 1] + len(plan(None, g - 1))
        assert counts[3] - counts[1] == 2 * STRIPS

        def before(i, c):
            if i is None:
                return counts[c]
            return counts[1] + (2 * i + c - 1) * STRIPS

        def group(i, c):
            return c if i is None else 2 * i + c

        def slot_round(i, c):
            return c // 2 if i is None else i + c // 2

        def steps(engine, step):
            step(None, 0)
            with engine.Fori(0, LOOPS) as i:
                step(i, 1)
                step(i, 2)
            for g in range(GROUPS - 3, GROUPS):
                step(None, g)

        def strip_bank(i, c, n):
            return 5 - n % 6 if i is None and c == -1 else 4 + n % 2

        block = ctx.enter_context(nc.Block())

        @block.sync
        def _(sp):
            def load_a(i, c):
                sp.dma_start(ka[:, c % 2, :, :], k_d[group(i, c)]).then_inc(a_loaded[c % 2], 16)
                if i is None and c < 2:
                    sp.wait_ge(qa_zeroed, c + 1)
                for odd in range(2):
                    sp.dma_start(qa[64 * odd:64 * odd + 64, c % 2, odd::2, :],
                                 q_one[group(i, c), odd]).then_inc(a_loaded[c % 2], 16)

            def load_b(i, c):
                sp.dma_start(qb[:, c % 2, :, :], q_d[group(i, c)]).then_inc(b_loaded[c % 2], 16)
                for odd in range(2):
                    sp.dma_start(kb[64 * odd:64 * odd + 64, c % 2, odd::2, :],
                                 k_one[group(i, c), odd]).then_inc(b_loaded[c % 2], 16)
                sp.dma_start(v_in[:, c % 2, :, :, :], v_d[group(i, c)]).then_inc(v_loaded[c % 2], 16)

            def place_max(i, c):
                sp.wait_ge(max_split, group(i, c) + 1)
                sp.wait_ge(b_loaded[c % 2], 48 * (slot_round(i, c) + 1))
                sp.sem_inc(sp_turn, 1)
                for h in range(4):
                    for k in range(3):
                        row = 64 * (h % 2) + STACK * k + MAX_ROW
                        sp.dma_start(qb[row:row + 1, c % 2, h // 2, :],
                                     max_part[KT * h:KT * (h + 1), k, :]).then_inc(max_placed, 16)

            load_a(None, 0)
            load_a(None, 1)
            sp.wait_ge(kb_zeroed, 2)
            load_b(None, 0)
            place_max(None, 0)

            def step(i, c):
                g = c if i is None else None
                if g is None or g + 2 < GROUPS:
                    sp.wait_ge(strip_read, before(i, c))
                    sp.sem_inc(sp_turn, 1)
                    load_a(i, c + 2)
                if g is None or g + 1 < GROUPS:
                    if g != 0:
                        sp.wait_ge(pv_done, KT * group(i, c))
                        sp.sem_inc(sp_turn, 1)
                    load_b(i, c + 1)
                    place_max(i, c + 1)

            expert_loads = [(keep["wo"][:], w["wo_T"]), (keep["rms2_col"][:], w["ln2_col"]),
                            (keep["router"][:], w["gate_w_T"]),
                            (keep["expert_no"][:], w["expert_no"].partition_broadcast(P)),
                            (keep["w1"][:], w["w1_T"]), (keep["w3"][:], w["w3_T"]), (keep["w2"][:], w["w2_T"])]
            for dst, src in expert_loads:
                sp.dma_start(dst, src).then_inc(experts_loaded, 16)
            steps(sp, step)
            sp.wait_ge(experts_loaded, 16 * len(expert_loads))
            sp.wait_ge(max_placed, 16 * 12 * GROUPS)

        @block.gpsimd
        def _(pool):
            for slot in range(2):
                nc.gpsimd.memset(kb[:, slot, :, :], 0.0).then_inc(kb_zeroed, 1)
            nc.gpsimd.memset(v_pad[:], 1.0).then_inc(ones_ready, 1)
            pool.wait_ge(ones_ready, 1)

            def pad(i, c):
                pool.wait_ge(v_loaded[c % 2], 16 * (slot_round(i, c) + 1))
                pool.sem_inc(pool_turn, 1)
                nc.gpsimd.tensor_copy(v_pad[:, c % 2, :, :, 0:AD], v_in[:, c % 2, :, :, :]).then_inc(v_ready, 1)

            def step(i, c):
                if i is None and c == GROUPS - 1:
                    return
                if i is not None or c > 0:
                    pool.wait_ge(pv_done, KT * group(i, c))
                    pool.sem_inc(pool_turn, 1)
                pad(i, c + 1)

            pad(None, 0)
            steps(pool, step)

        @block.scalar
        def _(act):
            def step(i, c):
                for n in range(PER):
                    kt, h = n // 4, n % 4
                    act.wait_ge(scores_ready, group(i, c) * PER + n + 1)
                    used = kt - (1 if kt < KT % RING else RING - 1)
                    if i is not None or group(i, c) * KT + used > 0:
                        act.wait_ge(pv_done, group(i, c) * KT + used)
                    nc.scalar.activation(probs[:, kt % RING, h, :],
                                         bank[:, 2 * (n % 2):2 * (n % 2) + 2, :].rearrange("p a s -> p (a s)"),
                                         ACT.Exp).then_inc(probs_ready, 1)
                    if n in (3, 4) and (i is not None or c > 0):
                        copy_o(i, c - 1, n - 3)

            def copy_o(i, c, half):
                if half == 0:
                    act.wait_ge(first_half_done, group(i, c) + 1)
                else:
                    act.wait_ge(pv_done, KT * (group(i, c) + 1))
                nc.scalar.copy(o_sb[:, half * 512:(half + 1) * 512], bank[:, 6 + half, :]).then_inc(o_copied, 1)

            steps(act, step)
            copy_o(None, GROUPS - 1, 0)
            copy_o(None, GROUPS - 1, 1)

        @block.tensor
        def _(pe):
            MM, TR = nc.tensor.matmul, nc.tensor.transpose

            def fill(i, c, n, strip, wait):
                kind, of, j = strip
                if wait is not None:
                    pe.wait_ge(strip_read, wait)
                to = bank[:, strip_bank(i, c, n), :]
                if kind == "a":
                    if j in (0, AHEAD):
                        pe.wait_ge(a_loaded[of % 2], 48 * (slot_round(i, of) + 1))
                    h, qt, half = j // (2 * KT), j // 2 % KT, j % 2
                    last = MM(to, qa[:, of % 2, h, qt * P:(qt + 1) * P],
                              ka[:, of % 2, h // 2, half * 512:(half + 1) * 512], start=True, stop=True)
                elif kind == "m":
                    pe.wait_ge(maxT_wanted, group(i, of) + 1)
                    last = TR(to[0:PER, 0:P], neg_max[:, of % 2, :], ident[:])
                else:
                    pe.wait_ge(o_copied, 2 * group(i, of) + j + 1)
                    for k in range(4):
                        last = TR(to[:, k * P:(k + 1) * P], o_sb[:, (4 * j + k) * P:(4 * j + k + 1) * P], ident[:])
                last.then_inc(strip_filled, 1)

            def fills(i, c):
                base, out = before(i, c), []
                for n, strip in enumerate(plan(i, c)):
                    if i is None and c == -1:
                        need = n - 5 if n > 5 else None
                    else:
                        need = base + n - (1 if n else 0)
                    out.append((i, c, n, strip, need))
                return out

            def scores(i, c, n):
                kt, h = n // 4, n % 4
                if n == 0 and i is None and c == 0:
                    pe.wait_ge(strip_read, counts[0])
                if n == 0:
                    pe.wait_ge(b_loaded[c % 2], 48 * (slot_round(i, c) + 1))
                    pe.wait_ge(max_placed, 16 * 12 * (group(i, c) + 1))
                if i is not None or c > 0 or n >= 2:
                    pe.wait_ge(probs_ready, group(i, c) * PER + n - 1)
                for half in range(2):
                    last = MM(bank[:, 2 * (n % 2) + half, :], kb[:, c % 2, h, kt * P:(kt + 1) * P],
                              qb[:, c % 2, h // 2, half * 512:(half + 1) * 512], start=True, stop=True)
                last.then_inc(scores_ready, 1)

            def with_v(i, c, kt, quarter):
                if quarter == 0:
                    pe.wait_ge(probs_ready, group(i, c) * PER + 4 * kt + 4)
                if kt == 0 and quarter == 0:
                    pe.wait_ge(v_ready, group(i, c) + 1)
                if kt == 0 and quarter % 2 == 0 and (i is not None or c > 0):
                    pe.wait_ge(o_copied, 2 * group(i, c) - 1 + quarter // 2)
                for h in range(4):
                    at = quarter % 2 * QUARTER
                    last = MM(bank[32 * h:32 * h + 32, 6 + quarter // 2, at:at + QUARTER], v_pad[:, c % 2, kt, h, :],
                              probs[:, kt % RING, h, quarter * QUARTER:(quarter + 1) * QUARTER],
                              start=(kt == 0 and quarter % 2 == 0), stop=(kt == KT - 1 and quarter % 2 == 1))
                if quarter == 1 and kt == KT - 1:
                    last.then_inc(first_half_done, 1)
                if quarter == 3:
                    last.then_inc(pv_done, 1)

            for f in fills(None, -1):
                fill(*f)

            def step(i, c):
                todo = fills(i, c)
                g = c if i is None else None

                def fill_to(end, n):
                    while todo and todo[0][2] < end and not (todo[0][3][0] == "o" and n < 5):
                        fill(*todo.pop(0))

                for n in range(PER):
                    scores(i, c, n)
                    fill_to((2 * n + 1) * STRIPS // (2 * PER), n)
                    if n >= 5:
                        with_v(i, c, (n - 5) // 4, (n - 5) % 4)
                    elif g != 0:
                        with_v(i, c - 1, (n - 5) // 4 + KT, (n - 5) % 4)
                    fill_to((n + 1) * STRIPS // PER, n)
                assert not todo

            steps(pe, step)
            for n in range(5):
                with_v(None, GROUPS - 1, (n - 5) // 4 + KT, (n - 5) % 4)
            n = len(plan(None, GROUPS - 1))
            for half in range(2):
                fill(None, GROUPS - 1, half, ("o", GROUPS - 1, half), counts[GROUPS])

        @block.vector
        def _(dve):
            V = nc.vector

            def read(i, c, n, strip, at):
                kind, of, j = strip
                slot = of % 2
                dve.wait_ge(strip_filled, at + n + 1)
                frm = bank[:, strip_bank(i, c, n), :]
                if kind == "a":
                    V.tensor_reduce(row_max[:, slot, j % 2, j // 2:j // 2 + 1], frm, AXX, ALU.max).then_inc(strip_read, 1)
                elif kind == "m":
                    parts, rest = max_part, max_rest
                    order = 3 * group(i, of)
                    if i is not None or of > 0:
                        dve.wait_ge(max_placed, 16 * 12 * group(i, of))
                    V.tensor_copy(parts[:, 0, :], frm[0:PER, 0:P]).then_inc(dve_order, 1)
                    dve.wait_ge(dve_order, order + 2)
                    V.tensor_tensor(rest[:], frm[0:PER, 0:P], parts[:, 0, :], ALU.subtract).then_inc(strip_read, 1)
                    dve.wait_ge(strip_read, at + n + 1)
                    V.tensor_copy(parts[:, 1, :], rest[:]).then_inc(dve_order, 1)
                    dve.wait_ge(dve_order, order + 3)
                    V.tensor_tensor(parts[:, 2, :], rest[:], parts[:, 1, :], ALU.subtract).then_inc(max_split, 1)
                else:
                    outs = frm.rearrange("p (t h e) -> p t h e", t=4, h=4)
                    V.reciprocal(inv[:, j, :].rearrange("p (t h) -> p t h", t=4), outs[:, :, :, AD]).then_inc(inv_ready, 1)
                    dve.wait_ge(inv_ready, 2 * group(i, of) + j + 1)
                    g = group(i, of)
                    V.tensor_tensor(attn_g[:, bass.ds(g * KT * 4 * AD + j * 4 * 4 * AD, 4 * 4 * AD)]
                                    .rearrange("p (t h d) -> p t h d", t=4, h=4),
                                    outs[:, :, :, 0:AD],
                                    inv[:, j, :].rearrange("p (t h) -> p t h", t=4).unsqueeze(3)
                                    .to_broadcast([P, 4, 4, AD]), ALU.mult).then_inc(strip_read, 1)

            def combine(i, of, at, n):
                dve.wait_ge(strip_read, at + n)
                V.tensor_tensor(neg_max[:, of % 2, :], row_max[:, of % 2, 0, :], row_max[:, of % 2, 1, :],
                                ALU.max).then_inc(dve_order, 1)
                dve.wait_ge(dve_order, 3 * group(i, of) + 1)
                V.tensor_scalar(neg_max[:, of % 2, :], neg_max[:, of % 2, :], -1.0, None, ALU.mult).then_inc(maxT_wanted, 1)

            def step(i, c):
                at = before(i, c)
                strips = plan(i, c)
                for n, strip in enumerate(strips):
                    read(i, c, n, strip, at)
                    if strip[0] == "a" and strip[2] == TILES_A - 1:
                        combine(i, strip[1], at, n + 1)

            attn_g = attn[:].rearrange("p n d -> p (n d)")
            for slot in range(2):
                V.memset(qa[:, slot, :, :], 0.0).then_inc(qa_zeroed, 1)
            step(None, -1)
            steps(dve, step)
            for half in range(2):
                read(None, GROUPS - 1, half, ("o", GROUPS - 1, half), counts[GROUPS])


def experts_and_out(nc, keep, out):
    ctx = ExitStack()
    with ctx:
        def sb(name, shape, dt=F32):
            return ctx.enter_context(nc.sbuf_tensor(name, shape, dt))

        def sem(name):
            return ctx.enter_context(nc.semaphore(name))

        bank = ctx.enter_context(nc.psum_tensor("bank_d", [P, 8, 512], F32))
        x1_all = keep["x_all"][:].rearrange("p (b t) d -> p b t d", b=B)
        h2_all = keep["h2_all"][:].rearrange("p (b t) d -> p b t d", b=B)
        attn = keep["attn_all"][:].rearrange("p n d -> p (n d)").rearrange("p (b g t c) -> p b g t c", b=B, g=HG, t=NT)
        gate_rows, ident = keep["gate_rows"], keep["ident"]
        KB = FF // P
        AT = (0, 1, 3, 4)

        w1, w3, w2, wo = (keep[name] for name in ("w1", "w3", "w2", "wo"))
        router, rms2_col, expert_no = keep["router"], keep["rms2_col"], keep["expert_no"]
        eps = sb("eps_d", [P, 1])
        a_rows = sb("a_rows", [P, B, D])
        aT = sb("aT", [P, B, P])
        h3_next = sb("h3_next", [P, B, D])
        squares = sb("squares_d", [P, B, D])
        sumsq = sb("sumsq_d", [P, B])
        rms = sb("rms_d", [P, B])
        n3 = sb("n3", [P, B, D])
        n3T_next = sb("n3T_next", [P, B, P])
        n3T = sb("n3T", [P, B, P])
        logits = sb("logits", [P, B, NE])
        top = sb("top", [P, B, 8])
        top_at = sb("top_at", [P, B, 8], U32)
        top_no = sb("top_no", [P, B, 2])
        gap = sb("gap", [P, B])
        second = sb("second", [P, B])
        first_w = sb("first_w", [P, B])
        second_w = sb("second_w", [P, B])
        share1 = sb("share1", [P, B, NE])
        share_next = sb("share_next", [P, B, NE])
        share = sb("share", [P, B, NE])
        silu = sb("silu", [P, 2, B * P])
        hidden = sb("hidden", [P, 2, KB, B * P])
        acc = sb("acc", [P, B, D])
        result = sb("result", [P, B, D])

        attn_taken = sem("attn_taken")
        aT_ready = sem("aT_ready")
        aT_copied = sem("aT_copied")
        o_ready = sem("o_ready")
        h3_ready = sem("h3_ready")
        rms_ready = sem("rms3_ready")
        n3_ready = sem("n3_ready")
        n3T_ready = sem("n3T_ready")
        next_ready = sem("next_ready")
        logits_ready = sem("logits_ready")
        gap_ready = sem("gap_ready")
        eps_ready = sem("eps_ready")
        gated = sem("gated")
        second_ready = sem("second_ready")
        share_ready = sem("share_ready")
        n3T_set = sem("n3T_set")
        acc_set = sem("acc_set")
        up_ready = sem("up_ready")
        silu_ready = sem("silu_ready")
        hidden_ready = sem("hidden_ready")
        down_ready = sem("down_ready")
        added = sem("added")
        result_ready = sem("result_ready")
        stored = sem("stored")
        dve_order = sem("dve_order_d")
        act_order = sem("act_order_d")
        sp_turn = sem("sp_turn_d")
        dve_turn = sem("dve_turn_d")

        out_rows = out.rearrange("b (t p) d -> t p b d", p=P)

        def steps(engine, lead_up, main):
            for part in lead_up(0):
                part()
            with engine.Fori(0, NT - 1) as t:
                main(t, lead_up(t + 1))
            main(NT - 1, None)

        block = ctx.enter_context(nc.Block())

        @block.sync
        def _(sp):
            with sp.Fori(0, NT) as t:
                sp.wait_ge(result_ready, t + 1)
                sp.sem_inc(sp_turn, 1)
                sp.dma_start(out_rows[t], result[:]).then_inc(stored, 16)
            sp.wait_ge(stored, 16 * (NT + 1))

        @block.tensor
        def _(pe):
            MM, TR = nc.tensor.matmul, nc.tensor.transpose

            def lead_up(t):
                def turn_attention():
                    pe.wait_ge(attn_taken, t + 1)
                    for b in range(B):
                        last = TR(bank[:, 0, b * P:(b + 1) * P], a_rows[:, b, :], ident[:])
                    last.then_inc(aT_ready, 1)

                def project():
                    pe.wait_ge(aT_copied, t + 1)
                    for b in range(B):
                        last = MM(bank[:, 1, b * D:(b + 1) * D], aT[:, b, :], wo[:], start=True, stop=True)
                    last.then_inc(o_ready, 1)

                def turn_norm():
                    pe.wait_ge(n3_ready, t + 1)
                    for b in range(B):
                        last = TR(bank[:, 0, b * P:(b + 1) * P], n3[:, b, :], ident[:])
                    last.then_inc(n3T_ready, 1)

                def route():
                    pe.wait_ge(next_ready, t + 1)
                    for b in range(B):
                        last = MM(bank[:, 1, b * NE:(b + 1) * NE], n3T_next[:, b, :], router[:], start=True, stop=True)
                    last.then_inc(logits_ready, 1)

                return [turn_attention, project, turn_norm, route]

            def main(t, parts):
                def up(e):
                    for k in range(KB):
                        n = e * KB + k
                        pe.wait_ge(hidden_ready, t * NE * KB + n - 1 + 2)
                        for m, ws in enumerate((w1, w3)):
                            last = MM(bank[:, 2 + 2 * m + n % 2, :], ws[:, e, k * P:(k + 1) * P],
                                      n3T[:].rearrange("p b s -> p (b s)"), start=True, stop=True)
                            last.then_inc(up_ready, 1)

                def down(e):
                    pe.wait_ge(hidden_ready, t * NE * KB + (e + 1) * KB + 2)
                    pe.wait_ge(added, t * NE + e - 1 + 2)
                    for b in range(B):
                        for k in range(KB):
                            last = MM(bank[:, 6 + e % 2, b * D:(b + 1) * D], hidden[:, e % 2, k, b * P:(b + 1) * P],
                                      w2[:, e, k, :], start=(k == 0), stop=(k == KB - 1))
                    last.then_inc(down_ready, 1)

                pe.wait_ge(n3T_set, t + 1)
                for e in range(NE):
                    up(e)
                    if e:
                        down(e - 1)
                    if parts and e in AT:
                        parts[AT.index(e)]()
                down(NE - 1)

            steps(pe, lead_up, main)

        @block.scalar
        def _(act):
            A = nc.scalar.activation

            def lead_up(t):
                def take_attention():
                    for b in range(B):
                        last = nc.scalar.copy(a_rows[:, b, :].rearrange("p (g c) -> p g c", g=HG), attn[:, b, :, t, :])
                    last.then_inc(attn_taken, 1)

                def copy_turned():
                    act.wait_ge(aT_ready, t + 1)
                    nc.scalar.copy(aT[:].rearrange("p b s -> p (b s)"), bank[:, 0, :]).then_inc(aT_copied, 1)

                def root():
                    act.wait_ge(h3_ready, t + 1)
                    for b in range(B):
                        last = A(squares[:, b, :], h3_next[:, b, :], ACT.Square, accum_out=sumsq[:, b:b + 1])
                    last.then_inc(act_order, 1)
                    act.wait_ge(act_order, t * 2 + 1)
                    A(rms[:], sumsq[:], ACT.Ln, scale=1.0 / D, bias=eps[:]).then_inc(act_order, 1)
                    act.wait_ge(act_order, t * 2 + 2)
                    A(rms[:], rms[:], ACT.Exp, scale=-0.5).then_inc(rms_ready, 1)

                def scale_turned():
                    act.wait_ge(n3T_ready, t + 1)
                    A(n3T_next[:].rearrange("p b s -> p (b s)"), bank[:, 0, :], ACT.Copy,
                      scale=rms2_col[:, 0:1]).then_inc(next_ready, 1)

                def exp_gap():
                    act.wait_ge(gap_ready, t + 1)
                    A(second[:], gap[:], ACT.Exp).then_inc(second_ready, 1)

                return [take_attention, copy_turned, root, scale_turned, exp_gap]

            def main(t, parts):
                act.wait_ge(next_ready, t + 1)
                act.wait_ge(silu_ready, t * NE * KB + 1)
                nc.scalar.copy(n3T[:], n3T_next[:]).then_inc(n3T_set, 1)
                if parts:
                    parts[0]()
                for e in range(NE):
                    for k in range(KB):
                        n = e * KB + k
                        act.wait_ge(up_ready, 2 * (t * NE * KB + n + 1))
                        act.wait_ge(hidden_ready, t * NE * KB + n - 1 + 2)
                        A(silu[:, n % 2, :], bank[:, 2 + n % 2, :], ACT.Silu).then_inc(silu_ready, 1)
                    if parts and e in (0, 2, 3, 5):
                        parts[{0: 1, 2: 2, 3: 3, 5: 4}[e]]()

            act.sem_inc(silu_ready, 1)
            act.wait_ge(eps_ready, 1)
            steps(act, lead_up, main)

        @block.vector
        def _(dve):
            V = nc.vector
            V.memset(eps[:], RMS_EPS).then_inc(eps_ready, 1)
            dve.sem_inc(hidden_ready, 2)
            dve.sem_inc(added, 2)
            LEAD_STEPS = 8

            def lead_up(t):
                s = Steps(dve, dve_order, t * LEAD_STEPS)

                def then_settle(instruction):
                    s.add(instruction)
                    s.settle()

                def residual():
                    dve.wait_ge(o_ready, t + 1)
                    V.tensor_tensor(h3_next[:], h2_all[:, :, t, :],
                                    bank[:, 1, :].rearrange("p (b d) -> p b d", b=B), ALU.add).then_inc(h3_ready, 1)

                def norm():
                    dve.wait_ge(rms_ready, t + 1)
                    for b in range(B):
                        last = V.tensor_scalar(n3[:, b, :], h3_next[:, b, :], rms[:, b:b + 1], None, ALU.mult)
                    last.then_inc(n3_ready, 1)

                def top_two():
                    dve.wait_ge(logits_ready, t + 1)
                    then_settle(V.tensor_copy(logits[:], bank[:, 1, 0:B * NE].rearrange("p (b e) -> p b e", b=B)))
                    dve.sem_inc(dve_turn, 1)
                    for b in range(B):
                        last = V.max(top[:, b, :], logits[:, b, :])
                    then_settle(last)
                    dve.sem_inc(dve_turn, 1)
                    V.tensor_tensor(gap[:], top[:, :, 1], top[:, :, 0], ALU.subtract).then_inc(gap_ready, 1)
                    for b in range(B):
                        last = V.max_index(top_at[:, b, :], top[:, b, :], logits[:, b, :])
                    then_settle(last)
                    then_settle(V.tensor_copy(top_no[:], top_at[:, :, 0:2]))

                def shares():
                    dve.wait_ge(second_ready, t + 1)
                    then_settle(V.tensor_scalar(first_w[:], second[:], 1.0, None, ALU.add))
                    then_settle(V.reciprocal(first_w[:], first_w[:]))
                    then_settle(V.tensor_tensor(second_w[:], second[:], first_w[:], ALU.mult))
                    for b in range(B):
                        V.tensor_scalar(share1[:, b, :], expert_no[:], top_no[:, b, 0:1], first_w[:, b:b + 1],
                                        ALU.is_equal, ALU.mult)
                        last = V.tensor_scalar(share_next[:, b, :], expert_no[:], top_no[:, b, 1:2],
                                               second_w[:, b:b + 1], ALU.is_equal, ALU.mult)
                    then_settle(last)
                    V.tensor_tensor(share_next[:], share_next[:], share1[:], ALU.add).then_inc(share_ready, 1)
                    assert s.n == LEAD_STEPS, s.n

                return [residual, norm, top_two, shares]

            def main(t, parts):
                dve.wait_ge(share_ready, t + 1)
                dve.wait_ge(added, (t + 1) * NE + 2 - NE)
                V.tensor_copy(acc[:], h3_next[:])
                V.tensor_copy(share[:], share_next[:]).then_inc(acc_set, 1)
                dve.wait_ge(acc_set, t + 1)

                def add(e):
                    dve.wait_ge(down_ready, t * NE + e + 1)
                    if e:
                        dve.wait_ge(added, t * NE + e + 2)
                    for b in range(B):
                        last = V.scalar_tensor_tensor(out=acc[:, b, :], in0=bank[:, 6 + e % 2, b * D:(b + 1) * D],
                                                      scalar=share[:, b, e:e + 1], in1=acc[:, b, :],
                                                      op0=ALU.mult, op1=ALU.add)
                    last.then_inc(added, 1)

                for e in range(NE):
                    for k in range(KB):
                        n = e * KB + k
                        dve.wait_ge(silu_ready, t * NE * KB + n + 1 + 1)
                        V.tensor_tensor(hidden[:, e % 2, k, :], silu[:, n % 2, :], bank[:, 4 + n % 2, :],
                                        ALU.mult).then_inc(hidden_ready, 1)
                    if e:
                        add(e - 1)
                    if parts and e in (1, 2, 5, 6):
                        parts[{1: 0, 2: 1, 5: 2, 6: 3}[e]]()
                add(NE - 1)
                dve.wait_ge(added, (t + 1) * NE + 2)
                dve.wait_ge(stored, 16 * t + 16)
                V.tensor_tensor(result[:], acc[:], gate_rows[:, :, 3 * D:4 * D], ALU.mult).then_inc(gated, 1)
                dve.wait_ge(gated, t + 1)
                V.tensor_tensor(result[:], result[:], x1_all[:, :, t, :], ALU.add).then_inc(result_ready, 1)

            dve.sem_inc(stored, 16)
            steps(dve, lead_up, main)


def program(nc, w, out):
    with ExitStack() as ctx:
        def sb(name, shape, dt=F32):
            return ctx.enter_context(nc.sbuf_tensor(name, shape, dt))

        keep = {
            "x_all": sb("x_all", [P, TILES, D]),
            "h2_all": sb("h2_all", [P, TILES, D]),
            "gate_rows": sb("gate_rows", [P, B, 4 * D]),
            "ident": sb("ident", [P, P]),
        }
        scratch = {
            "q": nc.dram_tensor("q_stack", (B, AH, AD, STACK, L), BF16, kind="Internal").ap(),
            "k": nc.dram_tensor("k_stack", (B, AH, AD, STACK, L), BF16, kind="Internal").ap(),
            "v": nc.dram_tensor("v_groups", (B, HG, P, NT, 4 * AD), F32, kind="Internal").ap(),
        }
        state_space_and_qkv(nc, w, keep, scratch)
        keep["attn_all"] = sb("attn_all", [P, TILES, D])
        for name, shape in (("w1", [P, NE, FF]), ("w3", [P, NE, FF]), ("w2", [P, NE, FF // P, D]), ("wo", [P, D]),
                            ("router", [P, NE]), ("rms2_col", [P, 1]), ("expert_no", [P, NE])):
            keep[name] = sb(name, shape)
        attention(nc, w, keep, scratch)
        experts_and_out(nc, keep, out)


def kernel(**inputs):
    import ml_dtypes as _ml
    import numpy as _np
    import concourse.bacc as _bacc
    from concourse import mybir as _mybir
    from concourse.bass_utils import run_bass_kernel_spmd as _run

    bf16 = _np.dtype(_ml.bfloat16)
    laid = {}

    def put(name, a):
        laid[name] = _np.ascontiguousarray(a)

    put("u", inputs["L0_attn_u"])
    put("c_T", _np.asarray(inputs["L0_c"]).T)
    put("wmod", inputs["L0_wmod"])
    put("in_proj_T", _np.asarray(inputs["L0_attn_in_proj_w"]).T)
    put("out_proj_T", _np.asarray(inputs["L0_attn_out_proj_w"]).T)
    for name in ("conv_w", "dt_bias", "A_log"):
        put(name, inputs["L0_attn_" + name])
    put("conv_b_cols", _np.asarray(inputs["L0_attn_conv_b"]).reshape(4, P).T)
    put("ln_w_cols", _np.asarray(inputs["L0_attn_ln_w"]).reshape(2, P).T)
    put("ln1_col", _np.asarray(inputs["L0_ffn_ln1_w"]).reshape(P, 1))
    put("ln2_col", _np.asarray(inputs["L0_ffn_ln2_w"]).reshape(P, 1))
    for name in ("wq", "wk", "wv", "wo", "gate_w"):
        put(name + "_T", _np.asarray(inputs["L0_ffn_" + name]).T)
    put("w1_T", _np.asarray(inputs["L0_ffn_w1"]).transpose(2, 0, 1))
    put("w3_T", _np.asarray(inputs["L0_ffn_w3"]).transpose(2, 0, 1))
    put("w2_T", _np.asarray(inputs["L0_ffn_w2"]).reshape(NE, D, FF // P, P).transpose(3, 0, 2, 1))

    at = _np.arange(P)
    put("ident", _np.eye(P, dtype=_np.float32))
    put("ident_h", _np.eye(P, dtype=bf16))
    put("tri", _np.stack([at[:, None] <= at[None], at[:, None] > at[None],
                          _np.ones((P, P), bool)]).astype(_np.float32))
    put("neg_mask", _np.where(at[None] < at[:, None], -3e38, 0.0).astype(bf16))
    put("ones_h", _np.ones((3, B * P), bf16))
    put("expert_no", _np.arange(NE, dtype=_np.float32))
    put("neg_delta", _np.tile(_np.repeat(-_np.eye(NH), P, axis=1), (3, 1)).astype(bf16))
    pad = _np.zeros((AH, AD, STACK - MAX_ROW, L), bf16)
    put("q_pad", pad.reshape(P, STACK - MAX_ROW, L))
    pad = pad.copy()
    pad[:, 0:3, 0] = 1
    put("k_pad", pad.reshape(P, STACK - MAX_ROW, L))

    nc = _bacc.Bacc("TRN2", target_bir_lowering=False, num_devices=1)
    w = {k: nc.dram_tensor(f"in_{k}", a.shape, _mybir.dt.from_np(a.dtype), kind="ExternalInput").ap()
         for k, a in laid.items()}
    out = nc.dram_tensor("out_x", (B, L, D), F32, kind="ExternalOutput").ap()
    program(nc, w, out)
    r = _run(nc, [{f"in_{k}": a for k, a in laid.items()}], core_ids=[0])
    return r.results[0]["out_x"]
```
